# Optimizing a Trainium2 kernel written in Bass

```python
import numpy as np
import jax
import jax.numpy as jnp

def _softmax(x, axis=-1):
    return jax.nn.softmax(x, axis=axis)

def _gelu(x):
    return jax.nn.gelu(x, approximate=True)

def _silu(x):
    return jax.nn.silu(x)

def _sigmoid(x):
    return jax.nn.sigmoid(x)

def _layernorm(x, axis=-1, eps=1e-05):
    m = jnp.mean(x, axis=axis, keepdims=True)
    v = jnp.var(x, axis=axis, keepdims=True)
    return (x - m) / jnp.sqrt(v + eps)

def _scatter_add(tgt, idx, src, axis=0):
    return tgt.at[idx].add(src)

def _segment_sum(src, seg, n):
    return jax.ops.segment_sum(src, seg, n)
kernel_name = 'mk_flamingo_gated_d1_seqx_r4_33381a'

def setup_inputs(seed: int=0):
    np.random.seed(seed)
    _w = jnp.asarray

    def _rec_inputs():
        import jax
        import jax.numpy as jnp
        _rk = jax.random.key(seed)
        x = -0.0002928 + 1 * jax.random.normal(jax.random.fold_in(_rk, 1), (8, 512, 256), jnp.float32)
        _lenS = 512 - jax.random.randint(jax.random.fold_in(_rk, 7), (8,), 0, max(1, 512 // 4) + 1, jnp.int32)
        _lenS2 = 512 - jax.random.randint(jax.random.fold_in(_rk, 8), (8,), 0, max(1, 512 // 4) + 1, jnp.int32)
        _ctx_1024P = jax.random.normal(jax.random.fold_in(_rk, 11), (8, 16, 256), jnp.float32)
        _ctx_1024c = jax.random.dirichlet(jax.random.fold_in(_rk, 511), 0.3 * jnp.ones((16,), jnp.float32), (8, 512))
        _ctx_1024t = jnp.einsum('bsk,bkd->bsd', _ctx_1024c, _ctx_1024P)
        _ctx_1024t = _ctx_1024t * jax.lax.rsqrt(jnp.mean(jnp.square(_ctx_1024t)) + 1e-12) * 0.953939
        ctx_1024 = -1.39393e-06 + 0.999914 * (_ctx_1024t + 0.3 * jax.random.normal(jax.random.fold_in(_rk, 611), (8, 512, 256), jnp.float32))
        _g = jax.random.normal(jax.random.fold_in(_rk, 9001), (2, 1), jnp.float32)
        _g = jnp.sign(_g) * jnp.maximum(jnp.abs(_g), 1.0) + (_g == 0) * 1.0
        g_xattn = _g[0]
        g_ffn = _g[1]
        return (x, ctx_1024, g_xattn, g_ffn)
    x, ctx_1024, g_xattn, g_ffn = _rec_inputs()

    def _L0_xattn_setup():
        import jax, jax.numpy as jnp
        import numpy as np
        D_MODEL = 256
        N_HEADS = 16
        D_K = D_MODEL // N_HEADS
        WINDOW = 64
        B, S = (1, 1024)
        key = jax.random.key(seed)
        ks = jax.random.split(key, 11)
        sc = 1.0 / np.sqrt(D_MODEL)
        inp = {'query': jax.random.normal(ks[0], (B, S, D_MODEL), jnp.float32), 'key': jax.random.normal(ks[1], (B, S, D_MODEL), jnp.float32), 'value': jax.random.normal(ks[2], (B, S, D_MODEL), jnp.float32), 'Wq': jax.random.normal(ks[3], (D_MODEL, D_MODEL), jnp.float32) * sc, 'bq': jax.random.normal(ks[4], (D_MODEL,), jnp.float32) * 0.01, 'Wk': jax.random.normal(ks[5], (D_MODEL, D_MODEL), jnp.float32) * sc, 'bk': jax.random.normal(ks[6], (D_MODEL,), jnp.float32) * 0.01, 'Wv': jax.random.normal(ks[7], (D_MODEL, D_MODEL), jnp.float32) * sc, 'bv': jax.random.normal(ks[8], (D_MODEL,), jnp.float32) * 0.01, 'Wo': jax.random.normal(ks[9], (D_MODEL, D_MODEL), jnp.float32) * sc, 'bo': jax.random.normal(ks[10], (D_MODEL,), jnp.float32) * 0.01}
        return inp
    _L0_xattn_all = _L0_xattn_setup()
    _L0_xattn_in = {k: v for k, v in _L0_xattn_all.items() if k in ('Wq', 'bq', 'Wk', 'bk', 'Wv', 'bv', 'Wo', 'bo')}
    del _L0_xattn_all

    def _L0_ffn_setup():
        import jax, jax.numpy as jnp
        import numpy as np
        TOP_K = 2
        key = jax.random.key(seed)
        k1, k2, k3 = jax.random.split(key, 3)
        B, S, H, E = (4, 512, 256, 8)
        x = jax.random.normal(k1, (B, S, H), dtype=jnp.float32)
        gate_w = jax.random.normal(k2, (E, H), dtype=jnp.float32) / np.sqrt(H)
        gate_b = jnp.zeros((E,), dtype=jnp.float32)
        expert_w = jax.random.normal(k3, (E, H, H), dtype=jnp.float32) / np.sqrt(H)
        expert_b = jnp.zeros((E, H), dtype=jnp.float32)
        return {'x': x, 'gate_w': gate_w, 'gate_b': gate_b, 'expert_w': expert_w, 'expert_b': expert_b}
    _L0_ffn_all = _L0_ffn_setup()
    _L0_ffn_in = {k: v for k, v in _L0_ffn_all.items() if k in ('gate_w', 'gate_b', 'expert_w', 'expert_b')}
    del _L0_ffn_all
    return {'x': x, 'ctx_1024': ctx_1024, 'g_xattn': g_xattn, 'g_ffn': g_ffn, 'L0_xattn_Wq': _L0_xattn_in['Wq'], 'L0_xattn_bq': _L0_xattn_in['bq'], 'L0_xattn_Wk': _L0_xattn_in['Wk'], 'L0_xattn_bk': _L0_xattn_in['bk'], 'L0_xattn_Wv': _L0_xattn_in['Wv'], 'L0_xattn_bv': _L0_xattn_in['bv'], 'L0_xattn_Wo': _L0_xattn_in['Wo'], 'L0_xattn_bo': _L0_xattn_in['bo'], 'L0_ffn_gate_w': _L0_ffn_in['gate_w'], 'L0_ffn_gate_b': _L0_ffn_in['gate_b'], 'L0_ffn_expert_w': _L0_ffn_in['expert_w'], 'L0_ffn_expert_b': _L0_ffn_in['expert_b']}

def reference(x, ctx_1024, g_xattn, g_ffn, L0_xattn_Wq, L0_xattn_bq, L0_xattn_Wk, L0_xattn_bk, L0_xattn_Wv, L0_xattn_bv, L0_xattn_Wo, L0_xattn_bo, L0_ffn_gate_w, L0_ffn_gate_b, L0_ffn_expert_w, L0_ffn_expert_b):
    import jax
    import jax.numpy as jnp

    def _L0_xattn_ref(query, key, value, Wq, bq, Wk, bk, Wv, bv, Wo, bo):
        import jax, jax.numpy as jnp
        import numpy as np
        D_MODEL = 256
        N_HEADS = 16
        D_K = D_MODEL // N_HEADS
        WINDOW = 64
        B, S = (1, 1024)
        b, s, _ = query.shape

        def proj(x, W, bias):
            return (x @ W.T + bias).reshape(b, s, N_HEADS, D_K).transpose(0, 2, 1, 3)
        q = proj(query, Wq, bq)
        k = proj(key, Wk, bk)
        v = proj(value, Wv, bv)
        scores = jnp.einsum('bhqd,bhkd->bhqk', q, k) / np.sqrt(D_K)
        i = jnp.arange(s)[:, None]
        j = jnp.arange(s)[None, :]
        keep = (jnp.abs(i - j) <= WINDOW) & (j <= i)
        scores = jnp.where(keep[None, None], scores, -jnp.inf)
        attn = jax.nn.softmax(scores, axis=-1)
        out = jnp.einsum('bhqk,bhkd->bhqd', attn, v)
        out = out.transpose(0, 2, 1, 3).reshape(b, s, D_MODEL)
        return out @ Wo.T + bo

    def _L0_ffn_ref(x, gate_w, gate_b, expert_w, expert_b):
        import jax, jax.numpy as jnp
        import numpy as np
        TOP_K = 2
        gates = jax.nn.softmax(jnp.einsum('bsh,eh->bse', x, gate_w) + gate_b, axis=-1)
        top_gates, top_idx = jax.lax.top_k(gates, TOP_K)
        expert_out = jnp.einsum('bsh,eoh->bseo', x, expert_w) + expert_b
        selected = jnp.take_along_axis(expert_out, top_idx[..., None], axis=2)
        return (selected * top_gates[..., None]).sum(axis=2)
    x = x + jnp.tanh(g_xattn[0]) * _L0_xattn_ref(_layernorm(x, axis=-1), ctx_1024, ctx_1024, L0_xattn_Wq, L0_xattn_bq, L0_xattn_Wk, L0_xattn_bk, L0_xattn_Wv, L0_xattn_bv, L0_xattn_Wo, L0_xattn_bo)
    x = x + jnp.tanh(g_ffn[0]) * _L0_ffn_ref(_layernorm(x, axis=-1), L0_ffn_gate_w, L0_ffn_gate_b, L0_ffn_expert_w, L0_ffn_expert_b)
    return x

_drawn_inputs = setup_inputs


def setup_inputs(seed=0):
    import zlib

    import numpy as np

    out = dict(_drawn_inputs(seed))
    spreads = {'L0_ffn_gate_b': (0.0, 0.1), 'L0_ffn_expert_b': (0.0, 0.1)}
    factors = {'L0_xattn_bq': 5.884, 'L0_xattn_bk': 64.0, 'L0_xattn_bo': 3.989, 'L0_xattn_bv': 2.77}
    for name, (base, spread) in spreads.items():
        noise = np.random.default_rng([zlib.crc32(name.encode()), seed]).standard_normal(out[name].shape)
        drawn = base * np.exp(spread * noise) if base else spread * noise
        out[name] = jnp.asarray(drawn.astype(out[name].dtype))
    for name, factor in factors.items():
        out[name] = (out[name] * factor).astype(out[name].dtype)
    return out
```

```python
from contextlib import ExitStack

import concourse.bass as bass
from concourse import mybir

F32 = mybir.dt.float32
F16 = mybir.dt.float16
ALU = mybir.AluOpType
ACT = mybir.ActivationFunctionType
AX = mybir.AxisListType

P = 128
BLK = 64
EPS = 1e-5
WS = 64.0
MASKED = -61440.0
ONEHOT = 32768.0


def flamingo_layer(nc, x, ctx_in, g_xattn, g_ffn, Wq, bq, Wk, bk, Wv, bv, Wo, bo,
                   gate_w, gate_b, expert_w, expert_b, out):
    B, S, D = x.shape
    E = gate_w.shape[0]
    H = 16
    DK = D // H
    TP = S // P
    KC = D // P
    HH = H // KC
    NB = S // BLK
    V1 = DK + 1
    NEB = E * D // 512
    QS = WS * DK ** -0.5
    SC = WS * WS
    KW = BLK + S
    assert D == 2 * P and S == 4 * P and DK == 16 and E == 8 and P == 2 * BLK

    with ExitStack() as stack:
        def sb(name, shape, dt=F32):
            return stack.enter_context(nc.sbuf_tensor(name, shape, dt))

        def sem(name):
            return stack.enter_context(nc.semaphore(name))

        x_in = sb("x_in", [P, TP, D])
        c_in = sb("c_in", [P, TP, D])
        y1 = sb("y1", [P, TP, D])
        res = sb("res", [P, TP, D])
        att = sb("att", [P, TP, D])
        y2 = sb("y2", [P, TP, D])
        acc = sb("acc", [P, TP, D])
        y1T = sb("y1T", [P, 2, KC, S], F16)
        cT = sb("cT", [P, 2, KC, S], F16)
        attT = sb("attT", [P, 2, KC, S], F16)
        y2T = sb("y2T", [P, 2, KC, S], F16)
        qs = sb("qs", [P, 2, KC, S], F16)
        ks = sb("ks", [P, 2, KC, S], F16)
        q_op = sb("q_op", [P, H, S], F16)
        k_op = sb("k_op", [P, H * 2 * KW], F16)
        vv = sb("vv", [P, 2, TP, H, V1])
        pr = sb("pr", [P, 3, 2, 512])
        mx = sb("mx", [P, TP, H])
        mxT = sb("mxT", [H, 2, S], F16)
        zrow = sb("zrow", [2 * H, S], F16)
        w_in = sb("w_in", [P, 4, 2, D])
        e_in = sb("e_in", [P, E, 2, D])
        gw_in = sb("gw_in", [E, D])
        wT = sb("wT", [P, 2, 4, KC, D], F16)
        eT = sb("eT", [P, 2, KC, E * D], F16)
        gwT = sb("gwT", [P, 2, KC, E], F16)
        eb_in = sb("eb_in", [E, D])
        ebp = sb("ebp", [E, 2, D], F16)
        eb3 = sb("eb3", [3 * E, D], F16)
        ident = sb("ident", [P, P])
        ident16 = sb("ident16", [P, P], F16)
        tmpl_q = sb("tmpl_q", [P, BLK], F16)
        tmpl_k = sb("tmpl_k", [P, 3, BLK], F16)
        g_in = sb("g_in", [P, 2])
        tg = sb("tg", [P, 4])
        qkb = sb("qkb", [P, 2, KC])
        qkbs = sb("qkbs", [P, 2, KC])
        bv_b = sb("bv_b", [P, D])
        bvs = sb("bvs", [P, D])
        bo_b = sb("bo_b", [P, D])
        bot = sb("bot", [P, D])
        gb_b = sb("gb_b", [P, E])
        st1 = sb("st1", [P, TP, 6])
        st2 = sb("st2", [P, TP, 6])
        mv1 = sb("mv1", [P, TP, 2])
        mv2 = sb("mv2", [P, TP, 2])
        ve = sb("ve", [P, 2, TP])
        rs1 = sb("rs1", [P, TP])
        rs2 = sb("rs2", [P, TP])
        mhalf = sb("mhalf", [P, TP])
        epst = sb("epst", [P, TP])
        rden = sb("rden", [P, 2, HH])
        lg = sb("lg", [P, TP, E])
        lmx = sb("lmx", [P, TP])
        ls = sb("ls", [P, TP, E])
        ex = sb("ex", [P, TP, E])
        esum = sb("esum", [P, TP])
        erec = sb("erec", [P, TP])
        gtw = sb("gtw", [P, TP, E, E])
        geq = sb("geq", [P, TP, E, E])
        lower = sb("lower", [P, E, E])
        rank = sb("rank", [P, TP, E])
        gsel = sb("gsel", [P, TP, E])
        gt = sb("gt", [P, TP, E])
        gs = sb("gs", [P, TP, E])
        g3 = sb("g3", [P, TP, 3 * E], F16)
        g3T = sb("g3T", [3 * E, S], F16)
        tmp = sb("tmp", [P, 2, 2, 512])
        ps = stack.enter_context(nc.psum_tensor("ps", [P, 8, 512], F32))

        n_w, n_e, n_c, n_eb3 = sem("loaded_w"), sem("loaded_e"), sem("loaded_consts"), sem("loaded_eb3")
        s_wt, s_wh, s_wl = sem("w_transposed"), sem("w_hi"), sem("w_lo")
        s_pc, s_dc, s_tg, s_bo = sem("pool_consts"), sem("dve_consts"), sem("tanh_done"), sem("bo_scaled")
        s_ebh, s_km, s_qz = sem("expert_bias_split"), sem("key_masks"), sem("q_rows_zeroed")
        n_x, n_ctx = sem("loaded_x"), sem("loaded_ctx")
        s_mv1, s_y1, s_res = sem("stats1"), sem("y1_done"), sem("res_done")
        s_rs1, s_rs2 = sem("deviation1"), sem("deviation2")
        s_xt, s_ct = sem("y1_transposed"), sem("ctx_transposed")
        s_xh, s_xl, s_ch, s_cl = sem("y1T_hi"), sem("y1T_lo"), sem("cT_hi"), sem("cT_lo")
        s_q, s_k, s_v = sem("q_product"), sem("k_product"), sem("v_product")
        s_qh, s_ql, s_kh, s_kl = sem("q_hi"), sem("q_lo"), sem("k_hi"), sem("k_lo")
        s_vs = sem("v_stored")
        n_st, n_v2, n_mr = sem("stacked"), sem("v_shifted"), sem("max_rows")
        s_sc, s_mx = sem("scores"), sem("maxima")
        s_mt, s_mh, s_ml = sem("max_transposed"), sem("max_hi"), sem("max_lo")
        s_st, s_p, s_av, s_a = sem("scores_t"), sem("probs"), sem("av_product"), sem("att_done")
        s_at, s_ah, s_al = sem("att_transposed"), sem("attT_hi"), sem("attT_lo")
        s_wo, s_x1 = sem("wo_product"), sem("x1_done")
        s_mv2, s_y2 = sem("stats2"), sem("y2_done")
        s_yt, s_yh, s_yl = sem("y2_transposed"), sem("y2T_hi"), sem("y2T_lo")
        s_lg, s_lr, s_ls, s_ex = sem("logits"), sem("logits_read"), sem("logits_less_max"), sem("gate_exp")
        s_g, s_gT, s_gc = sem("gates_done"), sem("gates_transposed"), sem("gatesT_copied")
        s_b, s_ac = sem("bias_product"), sem("acc_started")
        s_mo = sem("expert_product")
        s_b0, s_b1 = sem("bank0_free"), sem("bank1_free")
        s_fin, n_out = sem("out_final"), sem("stored")
        c_st1, c_st2, s_rd = sem("vector_stats1"), sem("vector_stats2"), sem("vector_denominators")
        c_gate, c_moe = sem("vector_gate_chain"), sem("vector_expert_chain")
        c_ln1, c_ln2, c_fin = sem("pool_norm1"), sem("pool_norm2"), sem("pool_final")

        def after(eng, s, value):
            if not (isinstance(value, int) and value <= 0):
                eng.wait_ge(s, value)

        def tok(t, i):
            return t.rearrange("b (c p) d -> b p c d", p=P)[i]

        def window(h, b):
            at = (2 * h + b % 2) * KW + b * BLK
            return k_op[:, at:at + 2 * BLK]

        def q_block(h, b):
            return q_op[:, h, b * BLK:(b + 1) * BLK]

        WQ, WK, WV, WO = range(4)
        PASSES = [(0, 0), (0, 1), (1, 0)]
        NPREP = 4 + KC * NEB + 1
        N_POOL_CONSTS = 15

        block = stack.enter_context(nc.Block())

        @block.sync
        def _(sp):
            for n, w in ((WQ, Wq), (WK, Wk)):
                for k in range(KC):
                    sp.dma_start(w_in[:, n, k, :], w[k * P:(k + 1) * P, :].rearrange("(h d) i -> d h i", d=DK)).then_inc(n_w, 16)
            for n, w in ((WV, Wv), (WO, Wo)):
                sp.dma_start(w_in[:, n, :, :], w.rearrange("(k p) i -> p k i", p=P)).then_inc(n_w, 16)
            sp.dma_start(x_in[:], tok(x, 0)).then_inc(n_x, 16)
            sp.dma_start(c_in[:], tok(ctx_in, 0)).then_inc(n_ctx, 16)
            sp.dma_start(gw_in[:], gate_w).then_inc(n_e, 16)
            sp.dma_start(e_in[:], expert_w.rearrange("e (k p) i -> p e k i", p=P)).then_inc(n_e, 16)
            sp.wait_ge(s_ebh, 2)
            for r, part in enumerate((0, 1, 0)):
                sp.dma_start(eb3[r * E:(r + 1) * E, :], ebp[:, part, :]).then_inc(n_eb3, 16)

            def load_next(i):
                sp.wait_ge(s_res, i + 1)
                sp.dma_start(x_in[:], tok(x, i + 1)).then_inc(n_x, 16)
                sp.wait_ge(s_ct, KC * (i + 1))
                sp.dma_start(c_in[:], tok(ctx_in, i + 1)).then_inc(n_ctx, 16)

            def stack_operands(i):
                after(sp, s_st, 2 * TP * i)
                if isinstance(i, int) and i == 0:
                    sp.wait_ge(s_dc, 6)
                    sp.wait_ge(s_qz, 1)
                sp.dma_start(q_op[3 * DK:3 * DK + 2, :, :], zrow[:, :]).then_inc(n_st, 16)
                for j in range(KC):
                    heads = slice(j * HH, (j + 1) * HH)
                    sp.wait_ge(s_ql, KC * i + j + 1)
                    for r, part in enumerate((0, 0, 1)):
                        sp.dma_start(q_op[r * DK:(r + 1) * DK, heads, :], qs[:, part, j, :]).then_inc(n_st, 16)
                for j in range(KC):
                    sp.wait_ge(s_kl, KC * i + j + 1)
                    for r, part in enumerate((0, 1, 0)):
                        to = k_op[r * DK:(r + 1) * DK, :].rearrange("p (r c) -> p r c", c=KW)
                        sp.dma_start(to[:, 2 * HH * j:2 * HH * (j + 1), BLK:KW],
                                     ks[:, part, j, :].unsqueeze(1).to_broadcast([P, 2, S])).then_inc(n_st, 16)

            def shift_v(i):
                sp.wait_ge(s_vs, 2 * (i + 1))
                sp.dma_start(vv[BLK:P, 0, :, :, :], vv[0:BLK, 1, :, :, :]).then_inc(n_v2, 16)
                sp.dma_start(vv[0:BLK, 0, 1:TP, :, :], vv[BLK:P, 1, 0:TP - 1, :, :]).then_inc(n_v2, 16)

            def max_rows(i):
                sp.wait_ge(s_ml, i + 1)
                for part in range(2):
                    r = 3 * DK + part
                    sp.dma_start(q_op[r:r + 1, :, :], mxT[:, part, :]).then_inc(n_mr, 16)

            def store(j, t):
                sp.wait_ge(s_fin, TP * j + t + 3)
                sp.dma_start(tok(out, j)[:, t, :], acc[:, t, :]).then_inc(n_out, 16)

            def batch(i, experts, more):
                stack_operands(i)
                shift_v(i)
                if more:
                    load_next(i)
                if experts:
                    store(i - 1, 0)
                    store(i - 1, 1)
                max_rows(i)
                if experts:
                    store(i - 1, 2)
                    store(i - 1, 3)

            batch(0, False, True)
            with sp.Fori(1, B - 1) as i:
                batch(i, True, True)
            batch(B - 1, True, False)
            for t in range(TP):
                store(B - 1, t)
            sp.wait_ge(n_out, 16 * TP * B + 16)

        @block.tensor
        def _(pe):
            def prep(n, ins):
                if n >= 2:
                    pe.wait_ge(s_wl, n - 1)
                for col, src in ins:
                    r, w = src.shape
                    mm = pe.transpose(ps[0:w, n % 2, col:col + r], src, ident[0:r, 0:r])
                mm.then_inc(s_wt, 1)

            def transposes(bank, src, done):
                for k in range(KC):
                    for t in range(TP):
                        mm = pe.transpose(ps[:, bank + k, t * P:(t + 1) * P], src[:, t, k * P:(k + 1) * P], ident[:, :])
                    mm.then_inc(done, 1)

            def norm_transposes(i):
                pe.wait_ge(s_y1, TP * (i + 1))
                transposes(6, y1, s_xt)
                pe.wait_ge(n_ctx, 16 * (i + 1))
                transposes(2, c_in, s_ct)

            def projections(i):
                pe.wait_ge(s_xl, KC * (i + 1))
                after(pe, s_yl, KC * i)
                for j in range(KC):
                    n = 0
                    for k in range(KC):
                        for a, w in PASSES:
                            mm = pe.matmul(ps[:, 6 + j, :], wT[:, w, WQ, k, j * P:(j + 1) * P], y1T[:, a, k, :],
                                           start=n == 0, stop=n == 5)
                            n += 1
                    mm.then_inc(s_q, 1)
                pe.wait_ge(s_cl, KC * (i + 1))
                after(pe, s_lr, i)
                for j in range(KC):
                    n = 0
                    for k in range(KC):
                        for a, w in PASSES:
                            mm = pe.matmul(ps[:, 2 + j, :], wT[:, w, WK, k, j * P:(j + 1) * P], cT[:, a, k, :],
                                           start=n == 0, stop=n == 5)
                            n += 1
                    mm.then_inc(s_k, 1)
                after(pe, s_x1, 2 * i)
                for t in range(TP):
                    n = 0
                    for k in range(KC):
                        for a, w in PASSES:
                            mm = pe.matmul(ps[:, 4 + t // 2, (t % 2) * D:(t % 2 + 1) * D],
                                           cT[:, a, k, t * P:(t + 1) * P], wT[:, w, WV, k, :],
                                           start=n == 0, stop=n == 5)
                            n += 1
                    if t % 2:
                        mm.then_inc(s_v, 1)

            def gate_bias(i):
                pe.wait_ge(s_g, i)
                pe.wait_ge(s_kl, KC * (i + 1))
                for t in range(TP):
                    mm = pe.transpose(ps[0:3 * E, 3, :].bitcast(F16)[:, t * P:(t + 1) * P], g3[:, t, :], ident16[:, :])
                mm.then_inc(s_gT, 1)
                pe.wait_ge(s_gc, i)
                pe.wait_ge(s_vs, 2 * (i + 1))
                for t in range(TP):
                    mm = pe.matmul(ps[:, 4 + t // 2, (t % 2) * D:(t % 2 + 1) * D], g3T[:, t * P:(t + 1) * P], eb3[:, :],
                                   start=True, stop=True)
                    if t % 2:
                        mm.then_inc(s_b, 1)

            def experts(j, t, banks):
                for e in banks:
                    n = 2 * t + e // 2
                    pe.wait_ge((s_b0, s_b1)[e % 2], 2 * TP * j + n + 1)
                    m = 0
                    for k in range(KC):
                        for a, w in PASSES:
                            mm = pe.matmul(ps[:, e % 2, :], y2T[:, a, k, t * P:(t + 1) * P],
                                           eT[:, w, k, e * 512:(e + 1) * 512], start=m == 0, stop=m == 5)
                            m += 1
                    mm.then_inc(s_mo, 1)

            def first_pass(i, experts_before):
                pe.wait_ge(n_st, 16 * 13 * (i + 1))
                pe.wait_ge(s_vs, 2 * (i + 1))
                if experts_before:
                    pe.wait_ge(s_ac, 2 * i)
                for g in range(4 * TP):
                    c, hq = divmod(g, 4)
                    if g >= 4:
                        pe.wait_ge(s_mx, 4 * TP * i + g - 3)
                    for hh in range(4):
                        for par in range(2):
                            h, b = 4 * hq + hh, 2 * c + par
                            mm = pe.matmul(ps[BLK * par:BLK * (par + 1), 2 + g % 4, hh * P:(hh + 1) * P],
                                           q_block(h, b), window(h, b), start=True, stop=True)
                    mm.then_inc(s_sc, 1)

            def max_transposes(i):
                pe.wait_ge(s_mx, 4 * TP * (i + 1))
                for t in range(TP):
                    mm = pe.transpose(ps[0:H, 6, t * P:(t + 1) * P], mx[:, t, :], ident[:, :])
                mm.then_inc(s_mt, 1)

            def second_pass(i, u):
                c, half = divmod(u, 2)
                if u == 0:
                    pe.wait_ge(n_mr, 32 * (i + 1))
                if u >= 2:
                    pe.wait_ge(s_p, 2 * TP * i + u - 1)
                for hh in range(HH):
                    for par in range(2):
                        h, b = HH * half + hh, 2 * c + par
                        col = (2 * hh + par) * BLK
                        mm = pe.matmul(ps[:, 2 + 2 * (u % 2) + col // 512, col % 512:col % 512 + BLK],
                                       window(h, b), q_block(h, b), start=True, stop=True)
                mm.then_inc(s_st, 1)

            def values(i, u):
                c, half = divmod(u, 2)
                pe.wait_ge(s_p, 2 * TP * i + u + 1)
                if u == 0:
                    pe.wait_ge(n_v2, 32 * (i + 1))
                if u >= 2:
                    pe.wait_ge(s_a, 2 * TP * i + u - 1)
                for hh in range(HH):
                    mm = pe.matmul(ps[:, 6 + half, hh * 2 * V1:(hh + 1) * 2 * V1],
                                   pr[:, u % 3, hh // 4, (hh % 4) * P:(hh % 4 + 1) * P],
                                   vv[:, :, c, HH * half + hh, :], start=True, stop=True)
                mm.then_inc(s_av, 1)

            def output_projection(i):
                pe.wait_ge(s_al, KC * (i + 1))
                for t in range(TP):
                    n = 0
                    for k in range(KC):
                        for a, w in PASSES:
                            mm = pe.matmul(ps[:, 4 + t // 2, (t % 2) * D:(t % 2 + 1) * D],
                                           attT[:, a, k, t * P:(t + 1) * P], wT[:, w, WO, k, :],
                                           start=n == 0, stop=n == 5)
                            n += 1
                    if t % 2:
                        mm.then_inc(s_wo, 1)

            def gate_logits(i, more):
                pe.wait_ge(s_yl, KC * (i + 1))
                if more:
                    pe.wait_ge(s_cl, KC * (i + 2))
                for t in range(TP):
                    n = 0
                    for k in range(KC):
                        for a, w in PASSES:
                            mm = pe.matmul(ps[:, 2, t * E:(t + 1) * E], y2T[:, a, k, t * P:(t + 1) * P],
                                           gwT[:, w, k, :], start=n == 0, stop=n == 5)
                            n += 1
                mm.then_inc(s_lg, 1)

            def batch(i, with_experts, more):
                projections(i)
                if with_experts:
                    gate_bias(i)
                    experts(i - 1, 0, range(NEB))
                else:
                    pe.wait_ge(n_e, 32)
                    for n in range(5, NPREP):
                        eb, k = divmod(n - 5, KC)
                        prep(n, [(q * P, e_in[:, 2 * eb + q // 2, q % 2, k * P:(k + 1) * P]) for q in range(4)])
                    pe.wait_ge(s_wl, NPREP)
                    pe.wait_ge(n_eb3, 48)
                    pe.wait_ge(s_dc, 6)
                    pe.wait_ge(s_qz, 1)
                first_pass(i, with_experts)
                if with_experts:
                    experts(i - 1, 1, (0, 1))
                max_transposes(i)
                if with_experts:
                    experts(i - 1, 1, (2, 3))
                second_pass(i, 0)
                second_pass(i, 1)
                for u in range(2 * TP):
                    values(i, u)
                    if u + 2 < 2 * TP:
                        second_pass(i, u + 2)
                if with_experts:
                    experts(i - 1, 2, range(NEB))
                pe.wait_ge(s_a, 2 * TP * (i + 1))
                transposes(2, att, s_at)
                pe.wait_ge(s_al, KC * (i + 1))
                if more:
                    norm_transposes(i + 1)
                output_projection(i)
                if with_experts:
                    experts(i - 1, 3, range(NEB))
                pe.wait_ge(s_y2, TP * (i + 1))
                if more:
                    pe.wait_ge(s_xl, KC * (i + 2))
                transposes(6, y2, s_yt)
                gate_logits(i, more)

            pe.wait_ge(s_pc, N_POOL_CONSTS)
            pe.wait_ge(n_w, 96)
            for n in range(4):
                prep(n, [(k * D + o * P, w_in[:, n, o, k * P:(k + 1) * P]) for k in range(KC) for o in range(KC)])
            pe.wait_ge(n_e, 32)
            prep(4, [(k * E, gw_in[:, k * P:(k + 1) * P]) for k in range(KC)])
            norm_transposes(0)
            batch(0, False, True)
            with pe.Fori(1, B - 1) as i:
                batch(i, True, True)
            batch(B - 1, True, False)
            last = B
            pe.wait_ge(s_g, last)
            for t in range(TP):
                mm = pe.transpose(ps[0:3 * E, 3, :].bitcast(F16)[:, t * P:(t + 1) * P], g3[:, t, :], ident16[:, :])
            mm.then_inc(s_gT, 1)
            pe.wait_ge(s_gc, last)
            for t in range(TP):
                mm = pe.matmul(ps[:, 4 + t // 2, (t % 2) * D:(t % 2 + 1) * D], g3T[:, t * P:(t + 1) * P], eb3[:, :],
                               start=True, stop=True)
                if t % 2:
                    mm.then_inc(s_b, 1)
            for t in range(TP):
                experts(B - 1, t, range(NEB))

        @block.scalar
        def _(act):
            def high(dst, src, ready, count, done, scale=1.0, bias=0.0):
                act.wait_ge(ready, count)
                act.activation(dst, src, ACT.Identity, scale=scale, bias=bias).then_inc(done, 1)

            act.dma_start(g_in[:, 0:1], g_xattn.rearrange("(a b) -> a b", a=1).to_broadcast([P, 1])).then_inc(n_c, 16)
            act.dma_start(g_in[:, 1:2], g_ffn.rearrange("(a b) -> a b", a=1).to_broadcast([P, 1])).then_inc(n_c, 16)
            for dst, src, w in ((bv_b, bv, D), (bo_b, bo, D), (gb_b, gate_b, E)):
                act.dma_start(dst[:, :], src.rearrange("(a b) -> a b", a=1).to_broadcast([P, w])).then_inc(n_c, 16)
            with nc.allow_non_contiguous_dma(reason="256 biases into their partitions, once"):
                for n, src in ((0, bq), (1, bk)):
                    for j in range(KC):
                        act.dma_start(qkb[:, n, j:j + 1],
                                      src[j * P:(j + 1) * P].rearrange("(h d a) -> d h a", d=DK, a=1)).then_inc(n_c, 16)
            act.dma_start(eb_in[:, :], expert_b).then_inc(n_c, 16)
            act.wait_ge(n_c, 16 * 10)
            act.activation(tg[:, 0:2], g_in[:, :], ACT.Tanh).then_inc(s_tg, 1)
            act.activation(ebp[:, 0, :], eb_in[:, :], ACT.Identity).then_inc(s_ebh, 1)

            def prep_high(n):
                if n < 4:
                    high(wT[:, 0, n, :, :].rearrange("p k o -> p (k o)"), ps[:, n % 2, :], s_wt, n + 1, s_wh,
                         scale=QS if n == WQ else WS)
                elif n == 4:
                    high(gwT[:, 0, :, :].rearrange("p k o -> p (k o)"), ps[:, 0, 0:KC * E], s_wt, n + 1, s_wh, scale=WS)
                else:
                    eb, k = divmod(n - 5, KC)
                    high(eT[:, 0, k, eb * 512:(eb + 1) * 512], ps[:, n % 2, :], s_wt, n + 1, s_wh, scale=WS)

            def norm_high(i):
                for k in range(KC):
                    high(y1T[:, 0, k, :], ps[:, 6 + k, :], s_xt, KC * i + k + 1, s_xh)
                for k in range(KC):
                    high(cT[:, 0, k, :], ps[:, 2 + k, :], s_ct, KC * i + k + 1, s_ch)

            def experts(j, t, o):
                act.wait_ge(s_mo, TP * NEB * j + NEB * t + 2 * o + 2)
                if o == 0:
                    act.wait_ge(s_g, j + 1)
                    act.wait_ge(s_fin, TP * j + t + 1)
                for q in range(2):
                    e = 4 * o + 2 + q
                    a = act.activation(tmp[:, t % 2, o, q * D:(q + 1) * D], ps[:, 1, q * D:(q + 1) * D], ACT.Copy,
                                       scale=gs[:, t, e:e + 1])
                a.then_inc(s_b1, 1)

            def batch(i, with_experts, more):
                after(act, n_st, 16 * 13 * i)
                for j in range(KC):
                    high(qs[:, 0, j, :], ps[:, 6 + j, :], s_q, KC * i + j + 1, s_qh, bias=qkbs[:, 0, j:j + 1])
                for j in range(KC):
                    high(ks[:, 0, j, :], ps[:, 2 + j, :], s_k, KC * i + j + 1, s_kh, bias=qkbs[:, 1, j:j + 1])
                if with_experts:
                    act.wait_ge(s_gT, i)
                    act.activation(g3T[:, :], ps[0:3 * E, 3, :].bitcast(F16)[:, 0:S], ACT.Copy).then_inc(s_gc, 1)
                    experts(i - 1, 0, 0)
                    experts(i - 1, 0, 1)
                    experts(i - 1, 1, 0)
                else:
                    for n in range(5, NPREP):
                        prep_high(n)
                high(mxT[:, 0, :], ps[0:H, 6, :], s_mt, i + 1, s_mh, scale=1.0 / SC)
                if with_experts:
                    experts(i - 1, 1, 1)
                for u in range(2 * TP):
                    act.wait_ge(s_st, 2 * TP * i + u + 1)
                    if u >= 3:
                        act.wait_ge(s_av, 2 * TP * i + u - 2)
                    act.activation(pr[:, u % 3, :, :], ps[:, 2 + 2 * (u % 2):4 + 2 * (u % 2), :], ACT.Exp,
                                   scale=1.0 / SC).then_inc(s_p, 1)
                if with_experts:
                    experts(i - 1, 2, 0)
                    experts(i - 1, 2, 1)
                for k in range(KC):
                    high(attT[:, 0, k, :], ps[:, 2 + k, :], s_at, KC * i + k + 1, s_ah)
                if more:
                    norm_high(i + 1)
                if with_experts:
                    experts(i - 1, 3, 0)
                    experts(i - 1, 3, 1)
                for k in range(KC):
                    high(y2T[:, 0, k, :], ps[:, 6 + k, :], s_yt, KC * i + k + 1, s_yh)
                act.wait_ge(s_ls, i + 1)
                act.activation(ex[:, :, :], ls[:, :, :], ACT.Exp).then_inc(s_ex, 1)

            for n in range(5):
                prep_high(n)
            norm_high(0)
            act.wait_ge(s_dc, 5)
            batch(0, False, True)
            with act.Fori(1, B - 1) as i:
                batch(i, True, True)
            batch(B - 1, True, False)
            act.wait_ge(s_gT, B)
            act.activation(g3T[:, :], ps[0:3 * E, 3, :].bitcast(F16)[:, 0:S], ACT.Copy).then_inc(s_gc, 1)
            for t in range(TP):
                experts(B - 1, t, 0)
                experts(B - 1, t, 1)

        @block.vector
        def _(dve):
            class Chain:
                def __init__(self, s, per):
                    self.s, self.per, self.n = s, per, 0

                def begin(self, i):
                    self.i, self.n = i, 0

                def link(self, ins):
                    ins.then_inc(self.s, 1)
                    self.n += 1
                    dve.wait_ge(self.s, self.i * self.per + self.n)

                def end(self):
                    assert self.n == self.per, (self.n, self.per)

            gate_chain, moe_chain = Chain(c_gate, 11), Chain(c_moe, 2 * TP)

            def low(dst, src, hi, ready, count, done, scale=1.0, bias=None):
                dve.wait_ge(ready, count)
                if bias is not None:
                    dve.scalar_tensor_tensor(dst, src, bias, hi, ALU.add, ALU.subtract).then_inc(done, 1)
                elif scale != 1.0:
                    dve.scalar_tensor_tensor(dst, src, scale, hi, ALU.mult, ALU.subtract).then_inc(done, 1)
                else:
                    dve.tensor_tensor(dst, src, hi, ALU.subtract).then_inc(done, 1)

            def prep_low(n):
                if n < 4:
                    low(wT[:, 1, n, :, :].rearrange("p k o -> p (k o)"), ps[:, n % 2, :],
                        wT[:, 0, n, :, :].rearrange("p k o -> p (k o)"), s_wh, n + 1, s_wl, scale=QS if n == WQ else WS)
                elif n == 4:
                    low(gwT[:, 1, :, :].rearrange("p k o -> p (k o)"), ps[:, 0, 0:KC * E],
                        gwT[:, 0, :, :].rearrange("p k o -> p (k o)"), s_wh, n + 1, s_wl, scale=WS)
                else:
                    eb, k = divmod(n - 5, KC)
                    low(eT[:, 1, k, eb * 512:(eb + 1) * 512], ps[:, n % 2, :],
                        eT[:, 0, k, eb * 512:(eb + 1) * 512], s_wh, n + 1, s_wl, scale=WS)

            def norm_statistics(i):
                dve.wait_ge(n_x, 16 * (i + 1))
                for t in range(TP):
                    a = dve.bn_stats(st1[:, t, :], x_in[:, t, :])
                a.then_inc(c_st1, 1)
                dve.wait_ge(s_pc, 1)
                dve.wait_ge(c_st1, i + 1)
                for t in range(TP):
                    a = dve.bn_aggr(mv1[:, t, :], st1[:, t, :])
                a.then_inc(s_mv1, 1)

            def normalise(src, mv, rs, dst, done):
                for t in range(TP):
                    dve.tensor_scalar(dst[:, t, :], src[:, t, :], mv[:, t, 0:1], rs[:, t:t + 1],
                                      ALU.subtract, ALU.mult).then_inc(done, 1)

            def first_norm(i):
                after(dve, s_xt, KC * i)
                dve.wait_ge(s_rs1, i + 1)
                normalise(x_in, mv1, rs1, y1, s_y1)

            def second_norm(i):
                after(dve, s_yt, KC * i)
                dve.wait_ge(s_rs2, i + 1)
                normalise(res, mv2, rs2, y2, s_y2)

            def second_statistics(i):
                dve.wait_ge(s_x1, 2 * (i + 1))
                for t in range(TP):
                    a = dve.bn_stats(st2[:, t, :], res[:, t, :])
                a.then_inc(c_st2, 1)
                dve.wait_ge(s_pc, 1)
                dve.wait_ge(c_st2, i + 1)
                for t in range(TP):
                    a = dve.bn_aggr(mv2[:, t, :], st2[:, t, :])
                a.then_inc(s_mv2, 1)

            def norm_low(i):
                for k in range(KC):
                    low(y1T[:, 1, k, :], ps[:, 6 + k, :], y1T[:, 0, k, :], s_xh, KC * i + k + 1, s_xl)
                for k in range(KC):
                    low(cT[:, 1, k, :], ps[:, 2 + k, :], cT[:, 0, k, :], s_ch, KC * i + k + 1, s_cl)

            def gates(i):
                gate_chain.begin(i)
                link = gate_chain.link
                dve.wait_ge(s_lg, i + 1)
                link(dve.scalar_tensor_tensor(lg[:, :, :], ps[:, 2, 0:TP * E].rearrange("p (t e) -> p t e", e=E), 1.0 / WS,
                                              gb_b[:, :].unsqueeze(1).to_broadcast([P, TP, E]), ALU.mult, ALU.add))
                link(dve.tensor_reduce(lmx[:, :], lg[:, :, :], AX.X, ALU.max))
                dve.tensor_tensor(ls[:, :, :], lg[:, :, :], lmx[:, :].unsqueeze(2).to_broadcast([P, TP, E]),
                                  ALU.subtract).then_inc(s_ls, 1)
                dve.wait_ge(s_ex, i + 1)
                mine = ex[:, :, :].unsqueeze(3).to_broadcast([P, TP, E, E])
                other = ex[:, :, :].unsqueeze(2).to_broadcast([P, TP, E, E])
                dve.tensor_reduce(esum[:, :], ex[:, :, :], AX.X, ALU.add).then_inc(s_lr, 1)
                dve.tensor_tensor(gtw[:, :, :, :], other, mine, ALU.is_gt)
                link(dve.tensor_tensor(geq[:, :, :, :], other, mine, ALU.is_equal))
                link(dve.tensor_tensor(geq[:, :, :, :].rearrange("p t a b -> p t (a b)"),
                                       geq[:, :, :, :].rearrange("p t a b -> p t (a b)"),
                                       lower[:, :, :].rearrange("p a b -> p (a b)").unsqueeze(1).to_broadcast([P, TP, E * E]),
                                       ALU.mult))
                link(dve.tensor_tensor(gtw[:, :, :, :], gtw[:, :, :, :], geq[:, :, :, :], ALU.add))
                link(dve.tensor_reduce(rank[:, :, :], gtw[:, :, :, :], AX.X, ALU.add))
                link(dve.reciprocal(erec[:, :], esum[:, :]))
                link(dve.tensor_scalar(erec[:, :], erec[:, :], tg[:, 1:2], None, ALU.mult))
                link(dve.scalar_tensor_tensor(gsel[:, :, :], rank[:, :, :], 1.5, ex[:, :, :], ALU.is_lt, ALU.mult))
                link(dve.tensor_tensor(gt[:, :, :], gsel[:, :, :], erec[:, :].unsqueeze(2).to_broadcast([P, TP, E]),
                                       ALU.mult))
                dve.tensor_scalar(gs[:, :, :], gt[:, :, :], 1.0 / WS, None, ALU.mult)
                dve.tensor_copy(g3[:, :, 0:E], gt[:, :, :])
                link(dve.tensor_copy(g3[:, :, E:2 * E], gt[:, :, :]))
                dve.tensor_tensor(g3[:, :, 2 * E:3 * E], gt[:, :, :], g3[:, :, 0:E], ALU.subtract).then_inc(s_g, 1)
                gate_chain.end()

            def start_acc(i):
                dve.wait_ge(n_out, 16 * TP * (i - 1) + 16)
                for q in range(2):
                    dve.wait_ge(s_b, 2 * (i - 1) + q + 1)
                    dve.tensor_tensor(acc[:, 2 * q:2 * q + 2, :].rearrange("p t d -> p (t d)"), ps[:, 4 + q, :],
                                      res[:, 2 * q:2 * q + 2, :].rearrange("p t d -> p (t d)"), ALU.add).then_inc(s_ac, 1)

            def experts(j, t, o):
                dve.wait_ge(s_mo, TP * NEB * j + NEB * t + 2 * o + 1)
                if o == 0:
                    dve.wait_ge(s_g, j + 1)
                    dve.wait_ge(s_ac, 2 * j + t // 2 + 1)
                for q in range(2):
                    e = 4 * o + q
                    a = dve.scalar_tensor_tensor(acc[:, t, :], ps[:, 0, q * D:(q + 1) * D], gs[:, t, e:e + 1],
                                                 acc[:, t, :], ALU.mult, ALU.add)
                    if q == 0:
                        moe_chain.link(a)
                a.then_inc(s_b0, 1)
                if o == 0:
                    dve.wait_ge(s_b0, 2 * TP * j + 2 * t + 2)

            def batch(i, with_experts, more):
                for j in range(KC):
                    low(qs[:, 1, j, :], ps[:, 6 + j, :], qs[:, 0, j, :], s_qh, KC * i + j + 1, s_ql,
                        bias=qkbs[:, 0, j:j + 1])
                for j in range(KC):
                    low(ks[:, 1, j, :], ps[:, 2 + j, :], ks[:, 0, j, :], s_kh, KC * i + j + 1, s_kl,
                        bias=qkbs[:, 1, j:j + 1])
                after(dve, s_av, 2 * TP * i)
                for t in range(TP):
                    if t % 2 == 0:
                        dve.wait_ge(s_v, 2 * i + t // 2 + 1)
                    v = dve.tensor_tensor(vv[:, 1, t, :, 0:DK],
                                          ps[:, 4 + t // 2, (t % 2) * D:(t % 2 + 1) * D].rearrange("p (h d) -> p h d", h=H),
                                          bvs[:, :].rearrange("p (h d) -> p h d", h=H), ALU.add)
                    if t % 2:
                        v.then_inc(s_vs, 1)
                if with_experts:
                    start_acc(i)
                    moe_chain.begin(i - 1)
                    experts(i - 1, 0, 0)
                    experts(i - 1, 0, 1)
                else:
                    for n in range(5, NPREP):
                        prep_low(n)
                for g in range(4 * TP):
                    c, hq = divmod(g, 4)
                    dve.wait_ge(s_sc, 4 * TP * i + g + 1)
                    dve.tensor_reduce(mx[:, c, 4 * hq:4 * hq + 4], ps[:, 2 + g % 4, :].rearrange("p (h k) -> p h k", h=4),
                                      AX.X, ALU.max).then_inc(s_mx, 1)
                if with_experts:
                    experts(i - 1, 1, 0)
                dve.wait_ge(s_mh, i + 1)
                dve.scalar_tensor_tensor(mxT[:, 1, :], ps[0:H, 6, :], 1.0 / SC, mxT[:, 0, :], ALU.mult,
                                         ALU.subtract).then_inc(s_ml, 1)
                if with_experts:
                    experts(i - 1, 1, 1)
                if more:
                    norm_statistics(i + 1)
                    first_norm(i + 1)
                for u in range(2 * TP):
                    c, half = divmod(u, 2)
                    o = ps[:, 6 + half, 0:HH * 2 * V1].rearrange("p (h r v) -> p h r v", h=HH, r=2)
                    dve.wait_ge(s_av, 2 * TP * i + u + 1)
                    dve.reciprocal(rden[:, half, :], o[:, :, 1, DK]).then_inc(s_rd, 1)
                    dve.wait_ge(s_rd, 2 * TP * i + u + 1)
                    for r in range(2):
                        rows = slice(r * BLK, (r + 1) * BLK)
                        a = dve.tensor_tensor(
                            att[rows, c, half * P:(half + 1) * P].rearrange("p (h d) -> p h d", h=HH),
                            o[rows, :, r, 0:DK],
                            rden[rows, half, :].unsqueeze(2).to_broadcast([BLK, HH, DK]), ALU.mult)
                    a.then_inc(s_a, 1)
                if with_experts:
                    experts(i - 1, 2, 0)
                    experts(i - 1, 2, 1)
                for k in range(KC):
                    low(attT[:, 1, k, :], ps[:, 2 + k, :], attT[:, 0, k, :], s_ah, KC * i + k + 1, s_al)
                if more:
                    norm_low(i + 1)
                dve.wait_ge(s_res, i + 1)
                for q in range(2):
                    dve.wait_ge(s_wo, 2 * i + q + 1)
                    r = res[:, 2 * q:2 * q + 2, :].rearrange("p t d -> p (t d)")
                    dve.scalar_tensor_tensor(r, ps[:, 4 + q, :], tg[:, 2:3], r, ALU.mult, ALU.add).then_inc(s_x1, 1)
                second_statistics(i)
                if with_experts:
                    experts(i - 1, 3, 0)
                second_norm(i)
                if with_experts:
                    experts(i - 1, 3, 1)
                    moe_chain.end()
                for k in range(KC):
                    low(y2T[:, 1, k, :], ps[:, 6 + k, :], y2T[:, 0, k, :], s_yh, KC * i + k + 1, s_yl)
                gates(i)

            dve.wait_ge(s_pc, N_POOL_CONSTS)
            dve.memset(zrow[:, :], 0.0).then_inc(s_dc, 1)
            dve.memset(vv[:, 1, :, :, DK:V1], WS).then_inc(s_dc, 1)
            dve.memset(vv[0:BLK, 0, 0, :, :], 0.0).then_inc(s_b0, 1)
            dve.memset(acc[:, 0, 0:1], 0.0).then_inc(n_out, 16)
            norm_statistics(0)
            first_norm(0)
            for n in range(4):
                prep_low(n)
            dve.wait_ge(n_c, 16 * 10)
            dve.tensor_scalar(qkbs[:, 0, :], qkb[:, 0, :], QS, None, ALU.mult)
            dve.tensor_scalar(bvs[:, :], bv_b[:, :], WS, None, ALU.mult)
            dve.wait_ge(s_tg, 1)
            dve.tensor_scalar(bot[:, :], bo_b[:, :], tg[:, 0:1], None, ALU.mult).then_inc(s_bo, 1)
            dve.tensor_scalar(tg[:, 2:3], tg[:, 0:1], 1.0 / WS, None, ALU.mult).then_inc(s_dc, 1)
            dve.wait_ge(s_ebh, 1)
            dve.tensor_tensor(ebp[:, 1, :], eb_in[:, :], ebp[:, 0, :], ALU.subtract).then_inc(s_ebh, 1)
            prep_low(4)
            dve.tensor_copy(q_op[BLK:P, :, :].rearrange("p h (b q) -> p (h b) q", q=BLK),
                            tmpl_q[BLK:P, :].unsqueeze(1).to_broadcast([BLK, H * NB, BLK])).then_inc(s_dc, 1)
            dve.tensor_scalar(qkbs[:, 1, :], qkb[:, 1, :], WS, None, ALU.mult).then_inc(s_dc, 1)
            norm_low(0)
            k_all = k_op[:, :].rearrange("p (h r b k) -> p h r b k", h=H, r=2, k=BLK)
            dve.tensor_copy(k_all[0:BLK, :, :, :, :].rearrange("p h r b k -> p (h r b) k"),
                            tmpl_k[0:BLK, 2, :].unsqueeze(1).to_broadcast([BLK, 2 * H * KW // BLK, BLK]))
            for r in range(2):
                for role in range(2):
                    at = (r + role) % 2
                    dve.tensor_copy(k_all[BLK:P, :, r, at::2, :],
                                    tmpl_k[BLK:P, role, :].unsqueeze(1).unsqueeze(1).to_broadcast(
                                        [BLK, H, len(range(at, NB + 1, 2)), BLK])).then_inc(s_km, 1)
            dve.wait_ge(s_km, 4)
            dve.memset(k_all[BLK:P, :, 0, 0, :], MASKED).then_inc(s_dc, 1)
            batch(0, False, True)
            with dve.Fori(1, B - 1) as i:
                batch(i, True, True)
            batch(B - 1, True, False)
            start_acc(B)
            moe_chain.begin(B - 1)
            for t in range(TP):
                experts(B - 1, t, 0)
                experts(B - 1, t, 1)

        @block.gpsimd
        def _(pool):
            made = [0]

            def const(ins):
                ins.then_inc(s_pc, 1)
                made[0] += 1
                pool.wait_ge(s_pc, made[0])

            for t in (ident, ident16):
                const(pool.memset(t[:, :], 0.0))
                const(pool.affine_select(out=t[:, :], in_=t[:, :], compare_op=ALU.not_equal, fill=1.0, base=0,
                                         pattern=[[-1, P]], channel_multiplier=1))
            const(pool.memset(tmpl_q[:, :], 0.0))
            const(pool.affine_select(out=tmpl_q[:, :], in_=tmpl_q[:, :], compare_op=ALU.not_equal, fill=ONEHOT,
                                     base=-BLK, pattern=[[-1, BLK]], channel_multiplier=1))
            const(pool.memset(tmpl_k[:, :, :], 0.0))
            const(pool.affine_select(out=tmpl_k[:, 0, :], in_=tmpl_k[:, 0, :], compare_op=ALU.is_ge, fill=MASKED,
                                     base=BLK, pattern=[[1, BLK]], channel_multiplier=-1))
            const(pool.affine_select(out=tmpl_k[:, 1, :], in_=tmpl_k[:, 1, :], compare_op=ALU.is_ge, fill=MASKED,
                                     base=-BLK, pattern=[[-1, BLK]], channel_multiplier=1))
            for r in range(2):
                const(pool.affine_select(out=tmpl_k[:, 2, :], in_=tmpl_k[:, 2, :], compare_op=ALU.not_equal,
                                         fill=-SC, base=-(3 * DK + r), pattern=[[0, BLK]], channel_multiplier=1))
            const(pool.memset(lower[:, :, :], 1.0))
            const(pool.affine_select(out=lower[:, :, :], in_=lower[:, :, :], compare_op=ALU.is_gt, fill=0.0,
                                     base=0, pattern=[[1, E], [-1, E]], channel_multiplier=0))
            const(pool.memset(mhalf[:, :], -0.5))
            const(pool.memset(epst[:, :], EPS))
            pool.memset(q_op[BLK // 2:BLK, :, :], 0.0).then_inc(s_qz, 1)
            pool.wait_ge(s_qz, 1)
            pool.memset(tmp[:, 0, 0, 0:1], 0.0).then_inc(s_fin, 1)
            pool.memset(tmp[:, 0, 1, 0:1], 0.0).then_inc(s_fin, 1)
            pool.memset(tmp[:, 1, 1, 0:1], 0.0).then_inc(s_b1, 1)

            assert made[0] == N_POOL_CONSTS, made

            def deviation(i, mv, n, rs, chain, done):
                pool.tensor_tensor(ve[:, n, :], mv[:, :, 1], epst[:, :], ALU.add).then_inc(chain, 1)
                pool.wait_ge(chain, i + 1)
                pool.tensor_tensor(rs[:, :], ve[:, n, :], mhalf[:, :], ALU.pow).then_inc(done, 1)

            def first_norm(i):
                pool.wait_ge(s_mv1, i + 1)
                deviation(i, mv1, 0, rs1, c_ln1, s_rs1)

            def residual(i):
                after(pool, s_ac, 2 * i)
                pool.wait_ge(s_y1, TP * (i + 1))
                pool.tensor_tensor(res[:, :, :], x_in[:, :, :], bot[:, :].unsqueeze(1).to_broadcast([P, TP, D]),
                                   ALU.add).then_inc(s_res, 1)

            def experts(j, t):
                pool.wait_ge(s_b1, 2 * TP * j + 2 * t + 3)
                both = tmp[:, t % 2, 0, :]
                pool.tensor_tensor(both, both, tmp[:, t % 2, 1, :], ALU.add).then_inc(c_fin, 1)
                pool.wait_ge(c_fin, 2 * (TP * j + t) + 1)
                pool.wait_ge(s_b0, 2 * TP * j + 2 * t + 3)
                pool.tensor_tensor(acc[:, t, :], acc[:, t, :], both[:, 0:D], ALU.add).then_inc(c_fin, 1)
                pool.wait_ge(c_fin, 2 * (TP * j + t) + 2)
                pool.tensor_tensor(acc[:, t, :], acc[:, t, :], both[:, D:2 * D], ALU.add).then_inc(s_fin, 1)

            def batch(i, with_experts, more):
                residual(i)
                if with_experts:
                    experts(i - 1, 0)
                    experts(i - 1, 1)
                if more:
                    first_norm(i + 1)
                if with_experts:
                    experts(i - 1, 2)
                pool.wait_ge(s_mv2, i + 1)
                deviation(i, mv2, 1, rs2, c_ln2, s_rs2)
                if with_experts:
                    experts(i - 1, 3)

            first_norm(0)
            pool.wait_ge(s_bo, 1)
            batch(0, False, True)
            with pool.Fori(1, B - 1) as i:
                batch(i, True, True)
            batch(B - 1, True, False)
            for t in range(TP):
                experts(B - 1, t)


_INS = ['x', 'ctx_1024', 'g_xattn', 'g_ffn', 'L0_xattn_Wq', 'L0_xattn_bq', 'L0_xattn_Wk', 'L0_xattn_bk',
        'L0_xattn_Wv', 'L0_xattn_bv', 'L0_xattn_Wo', 'L0_xattn_bo', 'L0_ffn_gate_w', 'L0_ffn_gate_b',
        'L0_ffn_expert_w', 'L0_ffn_expert_b']


def kernel(**inputs):
    import numpy as _np
    import concourse.bacc as _bacc
    from concourse import mybir as _mybir
    from concourse.bass_utils import run_bass_kernel_spmd as _run

    nc = _bacc.Bacc("TRN2", target_bir_lowering=False, num_devices=1)
    arrays, args = {}, []
    for name in _INS:
        a = _np.ascontiguousarray(inputs[name])
        arrays[f"in_{name}"] = a
        args.append(nc.dram_tensor(f"in_{name}", a.shape, _mybir.dt.from_np(a.dtype), kind="ExternalInput").ap())
    args.append(nc.dram_tensor("out_0", inputs["x"].shape, _mybir.dt.float32, kind="ExternalOutput").ap())
    flamingo_layer(nc, *args)
    return _run(nc, [arrays], core_ids=[0]).results[0]["out_0"]
```

```python
from contextlib import ExitStack

import concourse.bass as bass
from concourse import mybir

F32 = mybir.dt.float32
F16 = mybir.dt.float16
ALU = mybir.AluOpType
ACT = mybir.ActivationFunctionType
AX = mybir.AxisListType

P = 128
BLK = 64
EPS = 1e-5
WS = 64.0
MASKED = -61440.0
ONEHOT = 32768.0


def flamingo_layer(nc, x, ctx_in, g_xattn, g_ffn, Wq, bq, Wk, bk, Wv, bv, Wo, bo,
                   gate_w, gate_b, expert_w, expert_b, out):
    B, S, D = x.shape
    E = gate_w.shape[0]
    H = 16
    DK = D // H
    TP = S // P
    KC = D // P
    HH = H // KC
    NB = S // BLK
    V1 = DK + 1
    NEB = E * D // 512
    QS = WS * DK ** -0.5
    SC = WS * WS
    KW = BLK + S
    assert D == 2 * P and S == 4 * P and DK == 16 and E == 8 and P == 2 * BLK

    with ExitStack() as stack:
        def sb(name, shape, dt=F32):
            return stack.enter_context(nc.sbuf_tensor(name, shape, dt))

        def sem(name):
            return stack.enter_context(nc.semaphore(name))

        x_in = sb("x_in", [P, TP, D])
        c_in = sb("c_in", [P, TP, D])
        y1 = sb("y1", [P, TP, D])
        res = sb("res", [P, TP, D])
        att = sb("att", [P, TP, D])
        y2 = sb("y2", [P, TP, D])
        acc = sb("acc", [P, TP, D])
        y1T = sb("y1T", [P, 2, KC, S], F16)
        cT = sb("cT", [P, 2, KC, S], F16)
        attT = sb("attT", [P, 2, KC, S], F16)
        y2T = sb("y2T", [P, 2, KC, S], F16)
        qs = sb("qs", [P, 2, KC, S], F16)
        ks = sb("ks", [P, 2, KC, S], F16)
        q_op = sb("q_op", [P, H, S], F16)
        k_op = sb("k_op", [P, H * 2 * KW], F16)
        vv = sb("vv", [P, 2, 2, TP, H, V1], F16)
        pf = sb("pf", [P, 2, 2 * 512])
        pr = sb("pr", [P, 3, 2, 2 * 512], F16)
        mx = sb("mx", [P, TP, H])
        mxT = sb("mxT", [H, 2, S], F16)
        zrow = sb("zrow", [2 * H, S], F16)
        w_in = sb("w_in", [P, 4, 2, D])
        e_in = sb("e_in", [P, E, 2, D])
        gw_in = sb("gw_in", [E, D])
        wT = sb("wT", [P, 2, 4, KC, D], F16)
        eT = sb("eT", [P, 2, KC, E * D], F16)
        gwT = sb("gwT", [P, 2, KC, E], F16)
        eb_in = sb("eb_in", [E, D])
        ebp = sb("ebp", [E, 2, D], F16)
        eb3 = sb("eb3", [3 * E, D], F16)
        ident = sb("ident", [P, P])
        ident16 = sb("ident16", [P, P], F16)
        tmpl_q = sb("tmpl_q", [P, BLK], F16)
        tmpl_k = sb("tmpl_k", [P, 3, BLK], F16)
        g_in = sb("g_in", [P, 2])
        tg = sb("tg", [P, 4])
        qkb = sb("qkb", [P, 2, KC])
        qkbs = sb("qkbs", [P, 2, KC])
        bv_c = sb("bv_c", [P, KC])
        bv_w = sb("bv_w", [P, KC, P])
        bv_p = sb("bv_p", [P, 2, KC, P], F16)
        bo_b = sb("bo_b", [P, D])
        bot = sb("bot", [P, D])
        gb_b = sb("gb_b", [P, E])
        st1 = sb("st1", [P, TP, 6])
        st2 = sb("st2", [P, TP, 6])
        mv1 = sb("mv1", [P, TP, 2])
        mv2 = sb("mv2", [P, TP, 2])
        ve = sb("ve", [P, 2, TP])
        rs1 = sb("rs1", [P, TP])
        rs2 = sb("rs2", [P, TP])
        mhalf = sb("mhalf", [P, TP])
        epst = sb("epst", [P, TP])
        rden = sb("rden", [P, 2, HH])
        lg = sb("lg", [P, TP, E])
        lmx = sb("lmx", [P, TP])
        ls = sb("ls", [P, TP, E])
        ex = sb("ex", [P, TP, E])
        esum = sb("esum", [P, TP])
        erec = sb("erec", [P, TP])
        gtw = sb("gtw", [P, TP, E, E])
        geq = sb("geq", [P, TP, E, E])
        lower = sb("lower", [P, E, E])
        rank = sb("rank", [P, TP, E])
        gsel = sb("gsel", [P, TP, E])
        gt = sb("gt", [P, TP, E])
        gs = sb("gs", [P, TP, E])
        g3 = sb("g3", [P, TP, 3 * E], F16)
        g3T = sb("g3T", [3 * E, S], F16)
        free = sb("free", [P, 4])
        ps = stack.enter_context(nc.psum_tensor("ps", [P, 8, 512], F32))

        n_w, n_e, n_c, n_eb3 = sem("loaded_w"), sem("loaded_e"), sem("loaded_consts"), sem("loaded_eb3")
        s_wt, s_wh, s_wl = sem("w_transposed"), sem("w_hi"), sem("w_lo")
        s_pc, s_dc, s_tg, s_bo = sem("pool_consts"), sem("dve_consts"), sem("tanh_done"), sem("bo_scaled")
        s_ebh, s_km, s_qz = sem("expert_bias_split"), sem("key_masks"), sem("q_rows_zeroed")
        s_bw, s_bh, s_bl, s_bp = sem("bv_wide"), sem("bv_hi"), sem("bv_lo"), sem("bv_product")
        n_x, n_ctx = sem("loaded_x"), sem("loaded_ctx")
        s_mv1, s_y1, s_res = sem("stats1"), sem("y1_done"), sem("res_done")
        s_rs1, s_rs2 = sem("deviation1"), sem("deviation2")
        s_xt, s_ct = sem("y1_transposed"), sem("ctx_transposed")
        s_xh, s_xl, s_ch, s_cl = sem("y1T_hi"), sem("y1T_lo"), sem("cT_hi"), sem("cT_lo")
        s_q, s_k, s_v = sem("q_product"), sem("k_product"), sem("v_product")
        s_qh, s_ql, s_kh, s_kl = sem("q_hi"), sem("q_lo"), sem("k_hi"), sem("k_lo")
        s_vh, s_vl = sem("v_hi"), sem("v_lo")
        n_st, n_v2, n_mr = sem("stacked"), sem("v_shifted"), sem("max_rows")
        s_sc, s_mx = sem("scores"), sem("maxima")
        s_mt, s_mh, s_ml = sem("max_transposed"), sem("max_hi"), sem("max_lo")
        s_st, s_ph, s_pf, s_pl = sem("scores_t"), sem("probs_hi"), sem("probs"), sem("probs_lo")
        s_av, s_a = sem("av_product"), sem("att_done")
        s_at, s_ah, s_al = sem("att_transposed"), sem("attT_hi"), sem("attT_lo")
        s_wo, s_x1 = sem("wo_product"), sem("x1_done")
        s_mv2, s_y2 = sem("stats2"), sem("y2_done")
        s_yt, s_yh, s_yl = sem("y2_transposed"), sem("y2T_hi"), sem("y2T_lo")
        s_lg, s_ls, s_ex, s_geq, s_cmp = (
            sem("logits"), sem("logits_less_max"), sem("gate_exp"), sem("experts_equal"), sem("experts_compared"))
        s_g, s_gT, s_gc = sem("gates_done"), sem("gates_transposed"), sem("gatesT_copied")
        s_b, s_ac = sem("bias_product"), sem("acc_started")
        s_mo = sem("expert_product")
        s_mb = sem("expert_bank_free")
        s_fin, n_out = sem("out_final"), sem("stored")
        c_st1, c_st2, s_rd = sem("vector_stats1"), sem("vector_stats2"), sem("vector_denominators")
        c_gate = sem("vector_gate_chain")
        c_ln1, c_ln2, c_cmp, c_fin = sem("pool_norm1"), sem("pool_norm2"), sem("pool_compare"), sem("pool_final")

        def after(eng, s, value):
            if not (isinstance(value, int) and value <= 0):
                eng.wait_ge(s, value)

        tmp = e_in[:, :, :, :].rearrange("p (u b) q d -> p u b (q d)", u=2)

        def tok(t, i):
            return t.rearrange("b (c p) d -> b p c d", p=P)[i]

        def window(h, b):
            at = (2 * h + b % 2) * KW + b * BLK
            return k_op[:, at:at + 2 * BLK]

        def q_block(h, b):
            return q_op[:, h, b * BLK:(b + 1) * BLK]

        WQ, WK, WV, WO = range(4)
        FIRST_BANKS = (4, 5, 6, 7)
        PASSES = [(0, 0), (0, 1), (1, 0)]
        NPREP = 4 + KC * NEB + 1
        N_POOL_CONSTS = 15

        block = stack.enter_context(nc.Block())

        @block.sync
        def _(sp):
            for n, w in ((WQ, Wq), (WK, Wk)):
                for k in range(KC):
                    sp.dma_start(w_in[:, n, k, :], w[k * P:(k + 1) * P, :].rearrange("(h d) i -> d h i", d=DK)).then_inc(n_w, 16)
            for n, w in ((WV, Wv), (WO, Wo)):
                sp.dma_start(w_in[:, n, :, :], w.rearrange("(k p) i -> p k i", p=P)).then_inc(n_w, 16)
            sp.dma_start(x_in[:], tok(x, 0)).then_inc(n_x, 16)
            sp.dma_start(c_in[:], tok(ctx_in, 0)).then_inc(n_ctx, 16)
            sp.dma_start(gw_in[:], gate_w).then_inc(n_e, 16)
            sp.dma_start(e_in[:], expert_w.rearrange("e (k p) i -> p e k i", p=P)).then_inc(n_e, 16)
            sp.wait_ge(s_ebh, 2)
            for r, part in enumerate((0, 1, 0)):
                sp.dma_start(eb3[r * E:(r + 1) * E, :], ebp[:, part, :]).then_inc(n_eb3, 16)

            def load_next(i):
                sp.wait_ge(s_res, i + 1)
                sp.dma_start(x_in[:], tok(x, i + 1)).then_inc(n_x, 16)
                sp.wait_ge(s_ct, KC * (i + 1))
                sp.dma_start(c_in[:], tok(ctx_in, i + 1)).then_inc(n_ctx, 16)

            def stack_q(i):
                for j in range(KC):
                    heads = slice(j * HH, (j + 1) * HH)
                    sp.wait_ge(s_ql, KC * i + j + 1)
                    for r, part in enumerate((0, 0, 1)):
                        sp.dma_start(q_op[r * DK:(r + 1) * DK, heads, :], qs[:, part, j, :]).then_inc(n_st, 16)

            def stack_k(i):
                after(sp, s_st, 2 * TP * i)
                if isinstance(i, int) and i == 0:
                    sp.wait_ge(s_dc, 6)
                    sp.wait_ge(s_qz, 1)
                sp.dma_start(q_op[3 * DK:3 * DK + 2, :, :], zrow[:, :]).then_inc(n_st, 16)
                for j in range(KC):
                    sp.wait_ge(s_kl, KC * i + j + 1)
                    for r, part in enumerate((0, 1, 0)):
                        to = k_op[r * DK:(r + 1) * DK, :].rearrange("p (r c) -> p r c", c=KW)
                        sp.dma_start(to[:, 2 * HH * j:2 * HH * (j + 1), BLK:KW],
                                     ks[:, part, j, :].unsqueeze(1).to_broadcast([P, 2, S])).then_inc(n_st, 16)

            def shift_v(i):
                sp.wait_ge(s_vl, 2 * (i + 1))
                sp.dma_start(vv[BLK:P, :, 0, :, :, :], vv[0:BLK, :, 1, :, :, :]).then_inc(n_v2, 16)
                sp.dma_start(vv[0:BLK, :, 0, 1:TP, :, :], vv[BLK:P, :, 1, 0:TP - 1, :, :]).then_inc(n_v2, 16)

            def max_rows(i):
                sp.wait_ge(s_ml, i + 1)
                for part in range(2):
                    r = 3 * DK + part
                    sp.dma_start(q_op[r:r + 1, :, :], mxT[:, part, :]).then_inc(n_mr, 16)

            def store(j, t):
                sp.wait_ge(s_fin, TP * j + t + 3)
                sp.dma_start(tok(out, j)[:, t, :], acc[:, t, :]).then_inc(n_out, 16)

            def batch(i, experts, more):
                if more:
                    load_next(i)
                max_rows(i)
                if experts:
                    store(i - 1, 0)
                    store(i - 1, 1)
                if more:
                    stack_k(i + 1)
                    stack_q(i + 1)
                if experts:
                    store(i - 1, 2)
                if more:
                    shift_v(i + 1)
                if experts:
                    store(i - 1, 3)

            stack_k(0)
            stack_q(0)
            shift_v(0)
            batch(0, False, True)
            with sp.Fori(1, B - 1) as i:
                batch(i, True, True)
            batch(B - 1, True, False)
            for t in range(TP):
                store(B - 1, t)
            sp.wait_ge(n_out, 16 * TP * B + 16)

        @block.tensor
        def _(pe):
            def prep(n, ins):
                if n >= 2:
                    pe.wait_ge(s_wl, n - 1)
                for col, src in ins:
                    r, w = src.shape
                    mm = pe.transpose(ps[0:w, n % 2, col:col + r], src, ident[0:r, 0:r])
                mm.then_inc(s_wt, 1)

            def transpose(bank, src, k, done):
                for t in range(TP):
                    mm = pe.transpose(ps[:, bank, t * P:(t + 1) * P], src[:, t, k * P:(k + 1) * P], ident[:, :])
                mm.then_inc(done, 1)

            def y1_transposes(i, k):
                pe.wait_ge(s_y1, TP * (i + 1))
                transpose(6 + k, y1, k, s_xt)

            def ctx_transposes(i):
                pe.wait_ge(n_ctx, 16 * (i + 1))
                for k in range(KC):
                    transpose(4 + k, c_in, k, s_ct)

            def project(bank, w, src, j, done):
                n = 0
                for k in range(KC):
                    for a, b in PASSES:
                        mm = pe.matmul(ps[:, bank + j, :], wT[:, b, w, k, j * P:(j + 1) * P], src[:, a, k, :],
                                       start=n == 0, stop=n == 5)
                        n += 1
                mm.then_inc(done, 1)

            def project_qk(i):
                pe.wait_ge(s_cl, KC * (i + 1))
                for j in range(KC):
                    project(4, WK, cT, j, s_k)
                pe.wait_ge(s_xl, KC * (i + 1))
                for j in range(KC):
                    project(6, WQ, y1T, j, s_q)

            def by_token(bank, src, w, done):
                for t in range(TP):
                    n = 0
                    for k in range(KC):
                        for a, b in PASSES:
                            mm = pe.matmul(ps[:, bank + t // 2, (t % 2) * D:(t % 2 + 1) * D],
                                           src[:, a, k, t * P:(t + 1) * P], wT[:, b, w, k, :],
                                           start=n == 0, stop=n == 5)
                            n += 1
                    if t % 2:
                        mm.then_inc(done, 1)

            def project_v(i):
                pe.wait_ge(s_ql, KC * (i + 1))
                by_token(6, cT, WV, s_v)

            def gates_transposed(j):
                pe.wait_ge(s_g, j + 1)
                for t in range(TP):
                    mm = pe.transpose(ps[0:3 * E, 2, :].bitcast(F16)[:, t * P:(t + 1) * P], g3[:, t, :], ident16[:, :])
                mm.then_inc(s_gT, 1)

            def gate_bias(j):
                pe.wait_ge(s_gc, j + 1)
                for t in range(TP):
                    mm = pe.matmul(ps[:, 3 - t // 2, (t % 2) * D:(t % 2 + 1) * D], g3T[:, t * P:(t + 1) * P], eb3[:, :],
                                   start=True, stop=True)
                    if t % 2:
                        mm.then_inc(s_b, 1)

            def experts(j, t, banks):
                for e in banks:
                    pe.wait_ge(s_mb, TP * NEB * j + NEB * t + e + 1)
                    m = 0
                    for k in range(KC):
                        for a, w in PASSES:
                            mm = pe.matmul(ps[:, e % 2, :], y2T[:, a, k, t * P:(t + 1) * P],
                                           eT[:, w, k, e * 512:(e + 1) * 512], start=m == 0, stop=m == 5)
                            m += 1
                    mm.then_inc(s_mo, 1)

            def first_pass(i, g):
                c, hq = divmod(g, 4)
                bank = FIRST_BANKS[g % 4]
                if g == 0:
                    pe.wait_ge(n_st, 16 * 13 * (i + 1))
                if g == 2:
                    pe.wait_ge(s_vl, 2 * (i + 1))
                if g >= 4:
                    pe.wait_ge(s_mx, 4 * TP * i + g - 3)
                for hh in range(4):
                    for par in range(2):
                        h, b = 4 * hq + hh, 2 * c + par
                        mm = pe.matmul(ps[BLK * par:BLK * (par + 1), bank, hh * P:(hh + 1) * P],
                                       q_block(h, b), window(h, b), start=True, stop=True)
                mm.then_inc(s_sc, 1)

            def max_transposes(i):
                pe.wait_ge(s_mx, 4 * TP * (i + 1))
                after(pe, s_ac, 2 * i)
                for t in range(TP):
                    mm = pe.transpose(ps[0:H, 2, t * P:(t + 1) * P], mx[:, t, :], ident[:, :])
                mm.then_inc(s_mt, 1)

            def second_pass(i, u):
                c, half = divmod(u, 2)
                if u == 0:
                    pe.wait_ge(n_mr, 32 * (i + 1))
                if u >= 2:
                    pe.wait_ge(s_pf, 2 * TP * i + u - 1)
                for hh in range(HH):
                    for par in range(2):
                        h, b = HH * half + hh, 2 * c + par
                        col = (2 * hh + par) * BLK
                        mm = pe.matmul(ps[:, 2 + 2 * (u % 2) + col // 512, col % 512:col % 512 + BLK],
                                       window(h, b), q_block(h, b), start=True, stop=True)
                mm.then_inc(s_st, 1)

            def values(i, u):
                c, half = divmod(u, 2)
                pe.wait_ge(s_pl, 2 * TP * i + u + 1)
                if u == 0:
                    pe.wait_ge(n_v2, 32 * (i + 1))
                if u >= 2:
                    pe.wait_ge(s_a, 2 * TP * i + u - 1)
                for hh in range(HH):
                    for n, (a, b) in enumerate(PASSES):
                        mm = pe.matmul(ps[:, 6 + half, hh * 2 * V1:(hh + 1) * 2 * V1],
                                       pr[:, u % 3, a, hh * P:(hh + 1) * P], vv[:, b, :, c, HH * half + hh, :],
                                       start=n == 0, stop=n == 2)
                mm.then_inc(s_av, 1)

            def output_projection(i):
                pe.wait_ge(s_al, KC * (i + 1))
                by_token(2, attT, WO, s_wo)

            def gate_logits(i, with_experts):
                pe.wait_ge(s_yl, KC * (i + 1))
                after(pe, s_mb, TP * NEB * i + 1 if with_experts else 0)
                for t in range(TP):
                    n = 0
                    for k in range(KC):
                        for a, w in PASSES:
                            mm = pe.matmul(ps[:, 0, t * E:(t + 1) * E], y2T[:, a, k, t * P:(t + 1) * P],
                                           gwT[:, w, k, :], start=n == 0, stop=n == 5)
                            n += 1
                mm.then_inc(s_lg, 1)

            def batch(i, with_experts, more):
                for g in range(4 if with_experts else 0, 4 * TP):
                    first_pass(i, g)
                    if with_experts:
                        if g in (5, 6, 10, 12):
                            experts(i - 1, 0, [(5, 6, 10, 12).index(g)])
                        if g == 7:
                            gates_transposed(i - 1)
                        if g == 9:
                            gate_bias(i - 1)
                        if g == 14:
                            experts(i - 1, 1, [0])
                max_transposes(i)
                if with_experts:
                    experts(i - 1, 1, [1, 2, 3])
                second_pass(i, 0)
                second_pass(i, 1)
                for u in range(2 * TP):
                    if with_experts and u % 2 == 0:
                        experts(i - 1, 2, [u // 2])
                    if u + 2 < 2 * TP:
                        second_pass(i, u + 2)
                    if with_experts and u == 2 * TP - 1:
                        experts(i - 1, 3, [0])
                    values(i, u)
                if more:
                    pe.wait_ge(s_a, 2 * TP * (i + 1) - 1)
                    y1_transposes(i + 1, 0)
                pe.wait_ge(s_a, 2 * TP * (i + 1))
                for k in range(KC):
                    transpose(2 + k, att, k, s_at)
                if more:
                    y1_transposes(i + 1, 1)
                    ctx_transposes(i + 1)
                output_projection(i)
                if more:
                    project_qk(i + 1)
                if with_experts:
                    experts(i - 1, 3, [1, 2, 3])
                pe.wait_ge(s_y2, TP * (i + 1))
                for k in range(KC):
                    transpose(2 + k, y2, k, s_yt)
                if more:
                    project_v(i + 1)
                gate_logits(i, with_experts)
                if more:
                    for g in range(4):
                        first_pass(i + 1, g)

            pe.wait_ge(s_pc, N_POOL_CONSTS)
            pe.wait_ge(n_w, 96)
            for n in range(4):
                prep(n, [(k * D + o * P, w_in[:, n, o, k * P:(k + 1) * P]) for k in range(KC) for o in range(KC)])
            pe.wait_ge(n_e, 32)
            prep(4, [(k * E, gw_in[:, k * P:(k + 1) * P]) for k in range(KC)])
            for k in range(KC):
                y1_transposes(0, k)
            ctx_transposes(0)
            project_qk(0)
            project_v(0)
            for n in range(5, NPREP):
                eb, k = divmod(n - 5, KC)
                prep(n, [(q * P, e_in[:, 2 * eb + q // 2, q % 2, k * P:(k + 1) * P]) for q in range(4)])
            pe.wait_ge(s_wl, NPREP)
            pe.wait_ge(s_bl, 1)
            n = 0
            for k in range(KC):
                for a, b in PASSES:
                    mm = pe.matmul(ps[:, 0, 0:D], bv_p[:, a, k, :], wT[:, b, WO, k, :], start=n == 0, stop=n == 5)
                    n += 1
            mm.then_inc(s_bp, 1)
            pe.wait_ge(n_eb3, 48)
            pe.wait_ge(s_dc, 6)
            pe.wait_ge(s_qz, 1)
            pe.wait_ge(s_bo, 1)
            batch(0, False, True)
            with pe.Fori(1, B - 1) as i:
                batch(i, True, True)
            batch(B - 1, True, False)
            gates_transposed(B - 1)
            gate_bias(B - 1)
            for t in range(TP):
                experts(B - 1, t, range(NEB))

        @block.scalar
        def _(act):
            def high(dst, src, ready, count, done, scale=1.0, bias=0.0):
                act.wait_ge(ready, count)
                act.activation(dst, src, ACT.Identity, scale=scale, bias=bias).then_inc(done, 1)

            act.dma_start(g_in[:, 0:1], g_xattn.rearrange("(a b) -> a b", a=1).to_broadcast([P, 1])).then_inc(n_c, 16)
            act.dma_start(g_in[:, 1:2], g_ffn.rearrange("(a b) -> a b", a=1).to_broadcast([P, 1])).then_inc(n_c, 16)
            for dst, src, w in ((bo_b, bo, D), (gb_b, gate_b, E)):
                act.dma_start(dst[:, :], src.rearrange("(a b) -> a b", a=1).to_broadcast([P, w])).then_inc(n_c, 16)
            with nc.allow_non_contiguous_dma(reason="256 biases into their partitions, once"):
                act.dma_start(bv_c[:, :], bv.rearrange("(k p) -> p k", p=P)).then_inc(n_c, 16)
                for n, src in ((0, bq), (1, bk)):
                    for j in range(KC):
                        act.dma_start(qkb[:, n, j:j + 1],
                                      src[j * P:(j + 1) * P].rearrange("(h d a) -> d h a", d=DK, a=1)).then_inc(n_c, 16)
            act.dma_start(eb_in[:, :], expert_b).then_inc(n_c, 16)
            act.wait_ge(n_c, 16 * 10)
            act.activation(tg[:, 0:2], g_in[:, :], ACT.Tanh).then_inc(s_tg, 1)
            act.activation(ebp[:, 0, :], eb_in[:, :], ACT.Identity).then_inc(s_ebh, 1)

            def prep_high(n):
                if n < 4:
                    high(wT[:, 0, n, :, :].rearrange("p k o -> p (k o)"), ps[:, n % 2, :], s_wt, n + 1, s_wh,
                         scale=QS if n == WQ else WS)
                elif n == 4:
                    high(gwT[:, 0, :, :].rearrange("p k o -> p (k o)"), ps[:, 0, 0:KC * E], s_wt, n + 1, s_wh, scale=WS)
                else:
                    eb, k = divmod(n - 5, KC)
                    high(eT[:, 0, k, eb * 512:(eb + 1) * 512], ps[:, n % 2, :], s_wt, n + 1, s_wh, scale=WS)

            def norm_high(i):
                for k in range(KC):
                    high(y1T[:, 0, k, :], ps[:, 6 + k, :], s_xt, KC * i + k + 1, s_xh)
                for k in range(KC):
                    high(cT[:, 0, k, :], ps[:, 4 + k, :], s_ct, KC * i + k + 1, s_ch)

            def experts(j, t, e):
                act.wait_ge(s_mo, TP * NEB * j + NEB * t + e + 1)
                if e == 0:
                    if t == 0:
                        act.wait_ge(s_g, j + 1)
                    act.wait_ge(s_fin, TP * j + t + 1)
                for q in range(2):
                    a = act.activation(tmp[:, t % 2, e, q * D:(q + 1) * D], ps[:, e % 2, q * D:(q + 1) * D], ACT.Copy,
                                       scale=gs[:, t, 2 * e + q:2 * e + q + 1])
                a.then_inc(s_mb, 1)

            def qk_high(i):
                after(act, n_st, 16 * 13 * i)
                for j in range(KC):
                    high(ks[:, 0, j, :], ps[:, 4 + j, :], s_k, KC * i + j + 1, s_kh, bias=qkbs[:, 1, j:j + 1])
                for j in range(KC):
                    high(qs[:, 0, j, :], ps[:, 6 + j, :], s_q, KC * i + j + 1, s_qh, bias=qkbs[:, 0, j:j + 1])

            def v_high(i):
                after(act, s_av, 2 * TP * i)
                for q in range(2):
                    high(vv[:, 0, 1, 2 * q:2 * q + 2, :, 0:DK], ps[:, 6 + q, :].rearrange("p (t h d) -> p t h d", t=2, h=H),
                         s_v, 2 * i + q + 1, s_vh)

            def copy_gates(j):
                act.wait_ge(s_gT, j + 1)
                act.activation(g3T[:, :], ps[0:3 * E, 2, :].bitcast(F16)[:, 0:S], ACT.Copy).then_inc(s_gc, 1)

            def batch(i, with_experts, more):
                if with_experts:
                    experts(i - 1, 0, 0)
                    copy_gates(i - 1)
                    for e in range(1, NEB):
                        experts(i - 1, 0, e)
                    experts(i - 1, 1, 0)
                high(mxT[:, 0, :], ps[0:H, 2, :], s_mt, i + 1, s_mh, scale=1.0 / SC)
                if with_experts:
                    for e in range(1, NEB):
                        experts(i - 1, 1, e)
                for u in range(2 * TP):
                    act.wait_ge(s_st, 2 * TP * i + u + 1)
                    if u >= 3:
                        act.wait_ge(s_av, 2 * TP * i + u - 2)
                    src = ps[:, 2 + 2 * (u % 2):4 + 2 * (u % 2), :].rearrange("p b c -> p (b c)")
                    act.activation(pr[:, u % 3, 0, :], src, ACT.Exp, scale=1.0 / SC).then_inc(s_ph, 1)
                    if u >= 2:
                        act.wait_ge(s_pl, 2 * TP * i + u - 1)
                    act.activation(pf[:, u % 2, :], src, ACT.Exp, scale=1.0 / SC).then_inc(s_pf, 1)
                    if with_experts and u % 2 == 1:
                        experts(i - 1, 2, u // 2)
                if with_experts:
                    experts(i - 1, 3, 0)
                for k in range(KC):
                    high(attT[:, 0, k, :], ps[:, 2 + k, :], s_at, KC * i + k + 1, s_ah)
                if more:
                    norm_high(i + 1)
                    qk_high(i + 1)
                if with_experts:
                    for e in range(1, NEB):
                        experts(i - 1, 3, e)
                for k in range(KC):
                    high(y2T[:, 0, k, :], ps[:, 2 + k, :], s_yt, KC * i + k + 1, s_yh)
                if more:
                    v_high(i + 1)
                act.wait_ge(s_ls, i + 1)
                act.activation(ex[:, :, :], ls[:, :, :], ACT.Exp).then_inc(s_ex, 1)

            for n in range(4):
                prep_high(n)
            act.wait_ge(s_bw, 1)
            act.activation(bv_p[:, 0, :, :], bv_w[:, :, :], ACT.Identity).then_inc(s_bh, 1)
            prep_high(4)
            norm_high(0)
            act.wait_ge(s_dc, 5)
            qk_high(0)
            v_high(0)
            for n in range(5, NPREP):
                prep_high(n)
            batch(0, False, True)
            with act.Fori(1, B - 1) as i:
                batch(i, True, True)
            batch(B - 1, True, False)
            copy_gates(B - 1)
            for t in range(TP):
                for e in range(NEB):
                    experts(B - 1, t, e)

        @block.vector
        def _(dve):
            class Chain:
                def __init__(self, s, per):
                    self.s, self.per, self.n = s, per, 0

                def begin(self, i):
                    self.i, self.n = i, 0

                def link(self, ins):
                    ins.then_inc(self.s, 1)
                    self.n += 1
                    dve.wait_ge(self.s, self.i * self.per + self.n)

                def end(self):
                    assert self.n == self.per, (self.n, self.per)

            gate_chain = Chain(c_gate, 9)

            def low(dst, src, hi, ready, count, done, scale=1.0, bias=None):
                dve.wait_ge(ready, count)
                if bias is not None:
                    dve.scalar_tensor_tensor(dst, src, bias, hi, ALU.add, ALU.subtract).then_inc(done, 1)
                elif scale != 1.0:
                    dve.scalar_tensor_tensor(dst, src, scale, hi, ALU.mult, ALU.subtract).then_inc(done, 1)
                else:
                    dve.tensor_tensor(dst, src, hi, ALU.subtract).then_inc(done, 1)

            def prep_low(n):
                if n < 4:
                    low(wT[:, 1, n, :, :].rearrange("p k o -> p (k o)"), ps[:, n % 2, :],
                        wT[:, 0, n, :, :].rearrange("p k o -> p (k o)"), s_wh, n + 1, s_wl, scale=QS if n == WQ else WS)
                elif n == 4:
                    low(gwT[:, 1, :, :].rearrange("p k o -> p (k o)"), ps[:, 0, 0:KC * E],
                        gwT[:, 0, :, :].rearrange("p k o -> p (k o)"), s_wh, n + 1, s_wl, scale=WS)
                else:
                    eb, k = divmod(n - 5, KC)
                    low(eT[:, 1, k, eb * 512:(eb + 1) * 512], ps[:, n % 2, :],
                        eT[:, 0, k, eb * 512:(eb + 1) * 512], s_wh, n + 1, s_wl, scale=WS)

            def norm_statistics(i):
                dve.wait_ge(n_x, 16 * (i + 1))
                for t in range(TP):
                    a = dve.bn_stats(st1[:, t, :], x_in[:, t, :])
                a.then_inc(c_st1, 1)
                dve.wait_ge(s_pc, 1)
                dve.wait_ge(c_st1, i + 1)
                for t in range(TP):
                    a = dve.bn_aggr(mv1[:, t, :], st1[:, t, :])
                a.then_inc(s_mv1, 1)

            def normalise(src, mv, rs, dst, done):
                for t in range(TP):
                    dve.tensor_scalar(dst[:, t, :], src[:, t, :], mv[:, t, 0:1], rs[:, t:t + 1],
                                      ALU.subtract, ALU.mult).then_inc(done, 1)

            def first_norm(i):
                after(dve, s_xt, KC * i)
                dve.wait_ge(s_rs1, i + 1)
                normalise(x_in, mv1, rs1, y1, s_y1)

            def second_norm(i):
                after(dve, s_yt, KC * i)
                dve.wait_ge(s_rs2, i + 1)
                normalise(res, mv2, rs2, y2, s_y2)

            def second_statistics(i):
                dve.wait_ge(s_x1, 2 * (i + 1))
                for t in range(TP):
                    a = dve.bn_stats(st2[:, t, :], res[:, t, :])
                a.then_inc(c_st2, 1)
                dve.wait_ge(s_pc, 1)
                dve.wait_ge(c_st2, i + 1)
                for t in range(TP):
                    a = dve.bn_aggr(mv2[:, t, :], st2[:, t, :])
                a.then_inc(s_mv2, 1)

            def norm_low(i):
                for k in range(KC):
                    low(y1T[:, 1, k, :], ps[:, 6 + k, :], y1T[:, 0, k, :], s_xh, KC * i + k + 1, s_xl)
                for k in range(KC):
                    low(cT[:, 1, k, :], ps[:, 4 + k, :], cT[:, 0, k, :], s_ch, KC * i + k + 1, s_cl)

            def maximum(i, g):
                c, hq = divmod(g, 4)
                dve.wait_ge(s_sc, 4 * TP * i + g + 1)
                dve.tensor_reduce(mx[:, c, 4 * hq:4 * hq + 4], ps[:, FIRST_BANKS[g % 4], :].rearrange("p (h k) -> p h k", h=4),
                                  AX.X, ALU.max).then_inc(s_mx, 1)

            def gates(i, more):
                gate_chain.begin(i)
                link = gate_chain.link
                dve.wait_ge(s_lg, i + 1)
                link(dve.scalar_tensor_tensor(lg[:, :, :], ps[:, 0, 0:TP * E].rearrange("p (t e) -> p t e", e=E), 1.0 / WS,
                                              gb_b[:, :].unsqueeze(1).to_broadcast([P, TP, E]), ALU.mult, ALU.add))
                link(dve.tensor_reduce(lmx[:, :], lg[:, :, :], AX.X, ALU.max))
                dve.tensor_tensor(ls[:, :, :], lg[:, :, :], lmx[:, :].unsqueeze(2).to_broadcast([P, TP, E]),
                                  ALU.subtract).then_inc(s_ls, 1)
                if more:
                    maximum(i + 1, 0)
                dve.wait_ge(s_ex, i + 1)
                mine = ex[:, :, :].unsqueeze(3).to_broadcast([P, TP, E, E])
                other = ex[:, :, :].unsqueeze(2).to_broadcast([P, TP, E, E])
                dve.tensor_tensor(gtw[:, :, :, :], other, mine, ALU.is_gt)
                dve.tensor_tensor(geq[:, :, :, :], other, mine, ALU.is_equal).then_inc(s_geq, 1)
                link(dve.tensor_reduce(esum[:, :], ex[:, :, :], AX.X, ALU.add))
                link(dve.reciprocal(erec[:, :], esum[:, :]))
                dve.tensor_scalar(erec[:, :], erec[:, :], tg[:, 1:2], None, ALU.mult).then_inc(c_gate, 1)
                gate_chain.n += 1
                if more:
                    for g in range(1, 4):
                        maximum(i + 1, g)
                dve.wait_ge(s_cmp, i + 1)
                link(dve.tensor_reduce(rank[:, :, :], gtw[:, :, :, :], AX.X, ALU.add))
                link(dve.scalar_tensor_tensor(gsel[:, :, :], rank[:, :, :], 1.5, ex[:, :, :], ALU.is_lt, ALU.mult))
                link(dve.tensor_tensor(gt[:, :, :], gsel[:, :, :], erec[:, :].unsqueeze(2).to_broadcast([P, TP, E]),
                                       ALU.mult))
                dve.tensor_scalar(gs[:, :, :], gt[:, :, :], 1.0 / WS, None, ALU.mult)
                dve.tensor_copy(g3[:, :, 0:E], gt[:, :, :])
                link(dve.tensor_copy(g3[:, :, E:2 * E], gt[:, :, :]))
                dve.tensor_tensor(g3[:, :, 2 * E:3 * E], gt[:, :, :], g3[:, :, 0:E], ALU.subtract).then_inc(s_g, 1)
                gate_chain.end()

            def start_acc(j):
                dve.wait_ge(n_out, 16 * TP * j + 16)
                for q in range(2):
                    dve.wait_ge(s_b, 2 * j + q + 1)
                    dve.tensor_tensor(acc[:, 2 * q:2 * q + 2, :].rearrange("p t d -> p (t d)"), ps[:, 3 - q, :],
                                      res[:, 2 * q:2 * q + 2, :].rearrange("p t d -> p (t d)"), ALU.add).then_inc(s_ac, 1)

            def q_low(i):
                for j in range(KC):
                    low(qs[:, 1, j, :], ps[:, 6 + j, :], qs[:, 0, j, :], s_qh, KC * i + j + 1, s_ql,
                        bias=qkbs[:, 0, j:j + 1])

            def k_low(i):
                for j in range(KC):
                    low(ks[:, 1, j, :], ps[:, 4 + j, :], ks[:, 0, j, :], s_kh, KC * i + j + 1, s_kl,
                        bias=qkbs[:, 1, j:j + 1])

            def v_low(i):
                for q in range(2):
                    low(vv[:, 1, 1, 2 * q:2 * q + 2, :, 0:DK], ps[:, 6 + q, :].rearrange("p (t h d) -> p t h d", t=2, h=H),
                        vv[:, 0, 1, 2 * q:2 * q + 2, :, 0:DK], s_vh, 2 * i + q + 1, s_vl)

            def normalise_att(i, u):
                c, half = divmod(u, 2)
                o = ps[:, 6 + half, 0:HH * 2 * V1].rearrange("p (h r v) -> p h r v", h=HH, r=2)
                dve.wait_ge(s_av, 2 * TP * i + u + 1)
                dve.reciprocal(rden[:, half, :], o[:, :, 1, DK]).then_inc(s_rd, 1)
                dve.wait_ge(s_rd, 2 * TP * i + u + 1)
                for r in range(2):
                    rows = slice(r * BLK, (r + 1) * BLK)
                    a = dve.tensor_tensor(
                        att[rows, c, half * P:(half + 1) * P].rearrange("p (h d) -> p h d", h=HH),
                        o[rows, :, r, 0:DK],
                        rden[rows, half, :].unsqueeze(2).to_broadcast([BLK, HH, DK]), ALU.mult)
                a.then_inc(s_a, 1)

            def batch(i, with_experts, more):
                for g in range(4 if with_experts else 0, 4 * TP):
                    maximum(i, g)
                    if with_experts and g == 11:
                        start_acc(i - 1)
                dve.wait_ge(s_mh, i + 1)
                dve.scalar_tensor_tensor(mxT[:, 1, :], ps[0:H, 2, :], 1.0 / SC, mxT[:, 0, :], ALU.mult,
                                         ALU.subtract).then_inc(s_ml, 1)
                if more:
                    norm_statistics(i + 1)
                    first_norm(i + 1)
                for u in range(2 * TP):
                    if u >= 3:
                        dve.wait_ge(s_av, 2 * TP * i + u - 2)
                    low(pr[:, u % 3, 1, :], pf[:, u % 2, :], pr[:, u % 3, 0, :], s_pf, 2 * TP * i + u + 1, s_pl)
                    if u >= 1:
                        normalise_att(i, u - 1)
                normalise_att(i, 2 * TP - 1)
                for k in range(KC):
                    low(attT[:, 1, k, :], ps[:, 2 + k, :], attT[:, 0, k, :], s_ah, KC * i + k + 1, s_al)
                if more:
                    norm_low(i + 1)
                dve.wait_ge(s_res, i + 1)
                for q in range(2):
                    dve.wait_ge(s_wo, 2 * i + q + 1)
                    r = res[:, 2 * q:2 * q + 2, :].rearrange("p t d -> p (t d)")
                    dve.scalar_tensor_tensor(r, ps[:, 2 + q, :], tg[:, 2:3], r, ALU.mult, ALU.add).then_inc(s_x1, 1)
                second_statistics(i)
                if more:
                    k_low(i + 1)
                second_norm(i)
                if more:
                    q_low(i + 1)
                for k in range(KC):
                    low(y2T[:, 1, k, :], ps[:, 2 + k, :], y2T[:, 0, k, :], s_yh, KC * i + k + 1, s_yl)
                if more:
                    v_low(i + 1)
                gates(i, more)

            dve.wait_ge(s_pc, N_POOL_CONSTS)
            dve.memset(zrow[:, :], 0.0).then_inc(s_dc, 1)
            dve.memset(vv[:, 0, 1, :, :, DK:V1], WS)
            dve.memset(vv[:, 1, 1, :, :, DK:V1], 0.0)
            dve.memset(bv_w[:, :, :], 0.0).then_inc(s_dc, 1)
            dve.memset(vv[0:BLK, :, 0, 0, :, :], 0.0)
            dve.memset(acc[:, 0, 0:1], 0.0).then_inc(n_out, 16)
            norm_statistics(0)
            first_norm(0)
            for n in range(4):
                prep_low(n)
            dve.wait_ge(n_c, 16 * 10)
            dve.tensor_scalar(qkbs[:, 0, :], qkb[:, 0, :], QS, None, ALU.mult)
            dve.wait_ge(s_dc, 2)
            dve.tensor_tensor(bv_w[:, :, :], bv_w[:, :, :], bv_c[:, :].unsqueeze(2).to_broadcast([P, KC, P]),
                              ALU.add).then_inc(s_bw, 1)
            dve.wait_ge(s_tg, 1)
            dve.tensor_scalar(tg[:, 2:3], tg[:, 0:1], 1.0 / WS, None, ALU.mult).then_inc(s_dc, 1)
            dve.wait_ge(s_ebh, 1)
            dve.tensor_tensor(ebp[:, 1, :], eb_in[:, :], ebp[:, 0, :], ALU.subtract).then_inc(s_ebh, 1)
            dve.wait_ge(s_bh, 1)
            dve.tensor_tensor(bv_p[:, 1, :, :], bv_w[:, :, :], bv_p[:, 0, :, :], ALU.subtract).then_inc(s_bl, 1)
            prep_low(4)
            dve.tensor_copy(q_op[BLK:P, :, :].rearrange("p h (b q) -> p (h b) q", q=BLK),
                            tmpl_q[BLK:P, :].unsqueeze(1).to_broadcast([BLK, H * NB, BLK])).then_inc(s_dc, 1)
            dve.tensor_scalar(qkbs[:, 1, :], qkb[:, 1, :], WS, None, ALU.mult).then_inc(s_dc, 1)
            norm_low(0)
            k_all = k_op[:, :].rearrange("p (h r b k) -> p h r b k", h=H, r=2, k=BLK)
            dve.tensor_copy(k_all[0:BLK, :, :, :, :].rearrange("p h r b k -> p (h r b) k"),
                            tmpl_k[0:BLK, 2, :].unsqueeze(1).to_broadcast([BLK, 2 * H * KW // BLK, BLK]))
            for r in range(2):
                for role in range(2):
                    at = (r + role) % 2
                    dve.tensor_copy(k_all[BLK:P, :, r, at::2, :],
                                    tmpl_k[BLK:P, role, :].unsqueeze(1).unsqueeze(1).to_broadcast(
                                        [BLK, H, len(range(at, NB + 1, 2)), BLK])).then_inc(s_km, 1)
            dve.wait_ge(s_km, 4)
            dve.memset(k_all[BLK:P, :, 0, 0, :], MASKED).then_inc(s_dc, 1)
            k_low(0)
            q_low(0)
            v_low(0)
            for n in range(5, NPREP):
                prep_low(n)
            dve.wait_ge(s_bp, 1)
            dve.scalar_tensor_tensor(bo_b[:, :], ps[:, 0, 0:D], 1.0 / WS, bo_b[:, :], ALU.mult, ALU.add).then_inc(s_bo, 1)
            dve.wait_ge(s_bo, 1)
            dve.tensor_scalar(bot[:, :], bo_b[:, :], tg[:, 0:1], None, ALU.mult).then_inc(s_bo, 1)
            batch(0, False, True)
            with dve.Fori(1, B - 1) as i:
                batch(i, True, True)
            batch(B - 1, True, False)
            start_acc(B - 1)

        @block.gpsimd
        def _(pool):
            made = [0]

            def const(ins):
                ins.then_inc(s_pc, 1)
                made[0] += 1
                pool.wait_ge(s_pc, made[0])

            for t in (ident, ident16):
                const(pool.memset(t[:, :], 0.0))
                const(pool.affine_select(out=t[:, :], in_=t[:, :], compare_op=ALU.not_equal, fill=1.0, base=0,
                                         pattern=[[-1, P]], channel_multiplier=1))
            const(pool.memset(tmpl_q[:, :], 0.0))
            const(pool.affine_select(out=tmpl_q[:, :], in_=tmpl_q[:, :], compare_op=ALU.not_equal, fill=ONEHOT,
                                     base=-BLK, pattern=[[-1, BLK]], channel_multiplier=1))
            const(pool.memset(tmpl_k[:, :, :], 0.0))
            const(pool.affine_select(out=tmpl_k[:, 0, :], in_=tmpl_k[:, 0, :], compare_op=ALU.is_ge, fill=MASKED,
                                     base=BLK, pattern=[[1, BLK]], channel_multiplier=-1))
            const(pool.affine_select(out=tmpl_k[:, 1, :], in_=tmpl_k[:, 1, :], compare_op=ALU.is_ge, fill=MASKED,
                                     base=-BLK, pattern=[[-1, BLK]], channel_multiplier=1))
            for r in range(2):
                const(pool.affine_select(out=tmpl_k[:, 2, :], in_=tmpl_k[:, 2, :], compare_op=ALU.not_equal,
                                         fill=-SC, base=-(3 * DK + r), pattern=[[0, BLK]], channel_multiplier=1))
            const(pool.memset(lower[:, :, :], 1.0))
            const(pool.affine_select(out=lower[:, :, :], in_=lower[:, :, :], compare_op=ALU.is_gt, fill=0.0,
                                     base=0, pattern=[[1, E], [-1, E]], channel_multiplier=0))
            const(pool.memset(mhalf[:, :], -0.5))
            const(pool.memset(epst[:, :], EPS))
            pool.memset(q_op[BLK // 2:BLK, :, :], 0.0).then_inc(s_qz, 1)
            pool.wait_ge(s_qz, 1)
            pool.memset(free[:, 0:1], 0.0).then_inc(s_fin, 1)
            pool.memset(free[:, 1:2], 0.0).then_inc(s_fin, 1)
            pool.memset(free[:, 2:3], 0.0).then_inc(s_mb, 1)
            pool.memset(free[:, 3:4], 0.0).then_inc(s_mb, 1)

            assert made[0] == N_POOL_CONSTS, made

            def deviation(i, mv, n, rs, chain, done):
                pool.tensor_tensor(ve[:, n, :], mv[:, :, 1], epst[:, :], ALU.add).then_inc(chain, 1)
                pool.wait_ge(chain, i + 1)
                pool.tensor_tensor(rs[:, :], ve[:, n, :], mhalf[:, :], ALU.pow).then_inc(done, 1)

            def first_norm(i):
                pool.wait_ge(s_mv1, i + 1)
                deviation(i, mv1, 0, rs1, c_ln1, s_rs1)

            def residual(i):
                after(pool, s_ac, 2 * i)
                pool.wait_ge(s_y1, TP * (i + 1))
                pool.tensor_tensor(res[:, :, :], x_in[:, :, :], bot[:, :].unsqueeze(1).to_broadcast([P, TP, D]),
                                   ALU.add).then_inc(s_res, 1)

            def experts(j, t):
                first = 4 * (TP * j + t)
                pool.wait_ge(s_mb, TP * NEB * j + NEB * t + 4)
                pool.tensor_tensor(tmp[:, t % 2, 0, :], tmp[:, t % 2, 0, :], tmp[:, t % 2, 1, :], ALU.add).then_inc(c_fin, 1)
                pool.wait_ge(s_mb, TP * NEB * j + NEB * t + 6)
                pool.tensor_tensor(tmp[:, t % 2, 2, :], tmp[:, t % 2, 2, :], tmp[:, t % 2, 3, :], ALU.add).then_inc(c_fin, 1)
                pool.wait_ge(c_fin, first + 2)
                pool.tensor_tensor(tmp[:, t % 2, 0, :], tmp[:, t % 2, 0, :], tmp[:, t % 2, 2, :], ALU.add).then_inc(c_fin, 1)
                pool.wait_ge(c_fin, first + 3)
                pool.wait_ge(s_ac, 2 * j + t // 2 + 1)
                pool.tensor_tensor(acc[:, t, :], acc[:, t, :], tmp[:, t % 2, 0, 0:D], ALU.add).then_inc(c_fin, 1)
                pool.wait_ge(c_fin, first + 4)
                pool.tensor_tensor(acc[:, t, :], acc[:, t, :], tmp[:, t % 2, 0, D:2 * D], ALU.add).then_inc(s_fin, 1)

            def compare(i):
                pool.wait_ge(s_geq, i + 1)
                pool.tensor_tensor(geq[:, :, :, :].rearrange("p t a b -> p t (a b)"),
                                   geq[:, :, :, :].rearrange("p t a b -> p t (a b)"),
                                   lower[:, :, :].rearrange("p a b -> p (a b)").unsqueeze(1).to_broadcast([P, TP, E * E]),
                                   ALU.mult).then_inc(c_cmp, 1)
                pool.wait_ge(c_cmp, i + 1)
                pool.tensor_tensor(gtw[:, :, :, :], gtw[:, :, :, :], geq[:, :, :, :], ALU.add).then_inc(s_cmp, 1)

            def batch(i, with_experts, more):
                residual(i)
                if with_experts:
                    experts(i - 1, 0)
                if more:
                    first_norm(i + 1)
                if with_experts:
                    experts(i - 1, 1)
                    experts(i - 1, 2)
                pool.wait_ge(s_mv2, i + 1)
                deviation(i, mv2, 1, rs2, c_ln2, s_rs2)
                if with_experts:
                    experts(i - 1, 3)
                compare(i)

            first_norm(0)
            pool.wait_ge(s_bo, 2)
            batch(0, False, True)
            with pool.Fori(1, B - 1) as i:
                batch(i, True, True)
            batch(B - 1, True, False)
            for t in range(TP):
                experts(B - 1, t)


_INS = ['x', 'ctx_1024', 'g_xattn', 'g_ffn', 'L0_xattn_Wq', 'L0_xattn_bq', 'L0_xattn_Wk', 'L0_xattn_bk',
        'L0_xattn_Wv', 'L0_xattn_bv', 'L0_xattn_Wo', 'L0_xattn_bo', 'L0_ffn_gate_w', 'L0_ffn_gate_b',
        'L0_ffn_expert_w', 'L0_ffn_expert_b']


def kernel(**inputs):
    import numpy as _np
    import concourse.bacc as _bacc
    from concourse import mybir as _mybir
    from concourse.bass_utils import run_bass_kernel_spmd as _run

    nc = _bacc.Bacc("TRN2", target_bir_lowering=False, num_devices=1)
    arrays, args = {}, []
    for name in _INS:
        a = _np.ascontiguousarray(inputs[name])
        arrays[f"in_{name}"] = a
        args.append(nc.dram_tensor(f"in_{name}", a.shape, _mybir.dt.from_np(a.dtype), kind="ExternalInput").ap())
    args.append(nc.dram_tensor("out_0", inputs["x"].shape, _mybir.dt.float32, kind="ExternalOutput").ap())
    flamingo_layer(nc, *args)
    return _run(nc, [arrays], core_ids=[0]).results[0]["out_0"]
```

```python
from contextlib import ExitStack

import concourse.bass as bass
from concourse import mybir

F32 = mybir.dt.float32
F16 = mybir.dt.float16
ALU = mybir.AluOpType
ACT = mybir.ActivationFunctionType
AX = mybir.AxisListType

P = 128
BLK = 64
EPS = 1e-5
WS = 64.0
MASKED = -61440.0
ONEHOT = 32768.0


def flamingo_layer(nc, x, ctx_in, g_xattn, g_ffn, Wq, bq, Wk, bk, Wv, bv, Wo, bo,
                   gate_w, gate_b, expert_w, expert_b, out):
    B, S, D = x.shape
    E = gate_w.shape[0]
    H = 16
    DK = D // H
    TP = S // P
    KC = D // P
    HH = H // KC
    NB = S // BLK
    V1 = DK + 1
    NEB = E * D // 512
    QS = WS * DK ** -0.5
    SC = WS * WS
    KW = BLK + S
    assert D == 2 * P and S == 4 * P and DK == 16 and E == 8 and P == 2 * BLK

    with ExitStack() as stack:
        def sb(name, shape, dt=F32):
            return stack.enter_context(nc.sbuf_tensor(name, shape, dt))

        def sem(name):
            return stack.enter_context(nc.semaphore(name))

        x_in = sb("x_in", [P, TP, D])
        c_in = sb("c_in", [P, TP, D])
        y1 = sb("y1", [P, TP, D])
        res = sb("res", [P, TP, D])
        att = sb("att", [P, TP, D])
        y2 = sb("y2", [P, TP, D])
        acc = sb("acc", [P, TP, D])
        y1T = sb("y1T", [P, 2, KC, S], F16)
        cT = sb("cT", [P, 2, KC, S], F16)
        attT = sb("attT", [P, 2, KC, S], F16)
        y2T = sb("y2T", [P, 2, KC, S], F16)
        qs = sb("qs", [P, 2, KC, S], F16)
        ks = sb("ks", [P, 2, KC, S], F16)
        q_op = sb("q_op", [P, H, S], F16)
        k_op = sb("k_op", [P, H * 2 * KW], F16)
        vv = sb("vv", [P, 2, 2, TP, H, V1], F16)
        pf = sb("pf", [P, 2, 2 * 512])
        pr = sb("pr", [P, 3, 2, 2 * 512], F16)
        mx = sb("mx", [P, TP, H])
        mxT = sb("mxT", [H, 2, S], F16)
        zrow = sb("zrow", [2 * H, S], F16)
        w_in = sb("w_in", [P, 4, 2, D])
        e_in = sb("e_in", [P, E, 2, D])
        gw_in = sb("gw_in", [E, D])
        wT = sb("wT", [P, 2, 4, KC, D], F16)
        eT = sb("eT", [P, 2, KC, E * D], F16)
        gwT = sb("gwT", [P, 2, KC, E], F16)
        eb_in = sb("eb_in", [E, D])
        ebp = sb("ebp", [E, 2, D], F16)
        eb3 = sb("eb3", [3 * E, D], F16)
        ident = sb("ident", [P, P])
        ident16 = sb("ident16", [P, P], F16)
        tmpl_q = sb("tmpl_q", [P, BLK], F16)
        tmpl_k = sb("tmpl_k", [P, 3, BLK], F16)
        g_in = sb("g_in", [P, 2])
        tg = sb("tg", [P, 4])
        qkb = sb("qkb", [P, 2, KC])
        qkbs = sb("qkbs", [P, 2, KC])
        bv_c = sb("bv_c", [P, KC])
        bv_w = sb("bv_w", [P, KC, P])
        bv_p = sb("bv_p", [P, 2, KC, P], F16)
        bo_b = sb("bo_b", [P, D])
        bot = sb("bot", [P, D])
        gb_b = sb("gb_b", [P, E])
        st1 = sb("st1", [P, TP, 6])
        st2 = sb("st2", [P, TP, 6])
        mv1 = sb("mv1", [P, TP, 2])
        mv2 = sb("mv2", [P, TP, 2])
        ve = sb("ve", [P, 2, TP])
        rs1 = sb("rs1", [P, TP])
        rs2 = sb("rs2", [P, TP])
        mhalf = sb("mhalf", [P, TP])
        epst = sb("epst", [P, TP])
        rden = sb("rden", [P, 2, HH])
        lg = sb("lg", [P, TP, E])
        lmx = sb("lmx", [P, TP])
        ls = sb("ls", [P, TP, E])
        ex = sb("ex", [P, TP, E])
        esum = sb("esum", [P, TP])
        erec = sb("erec", [P, TP])
        gtw = sb("gtw", [P, TP, E, E])
        geq = sb("geq", [P, TP, E, E])
        lower = sb("lower", [P, E, E])
        rank = sb("rank", [P, TP, E])
        gsel = sb("gsel", [P, TP, E])
        gt = sb("gt", [P, TP, E])
        gs = sb("gs", [P, TP, E])
        g3 = sb("g3", [P, TP, 3 * E], F16)
        g3T = sb("g3T", [3 * E, S], F16)
        free = sb("free", [P, 4])
        ps = stack.enter_context(nc.psum_tensor("ps", [P, 8, 512], F32))

        n_w = [sem("loaded_wk"), sem("loaded_wq"), sem("loaded_wv"), sem("loaded_wo")]
        n_gw, n_e, n_eb3 = sem("loaded_gate_w"), sem("loaded_expert_w"), sem("loaded_eb3")
        n_c, n_s = sem("loaded_qkv_biases"), sem("loaded_small")
        s_wt, s_wh, s_wl = sem("w_transposed"), sem("w_hi"), sem("w_lo")
        s_pc, s_zr, s_kop, s_qop = sem("pool_consts"), sem("zeros_made"), sem("key_rows_made"), sem("query_rows_made")
        s_sb, s_tg, s_tgs, s_bo = sem("biases_scaled"), sem("tanh_done"), sem("tanh_scaled"), sem("bo_scaled")
        s_ebh, s_ebl = sem("expert_bias_hi"), sem("expert_bias_lo")
        s_bz, s_bw, s_bh, s_bl, s_bp = sem("bv_zeros"), sem("bv_wide"), sem("bv_hi"), sem("bv_lo"), sem("bv_product")
        n_x, n_ctx = sem("loaded_x"), sem("loaded_ctx")
        s_mv1, s_y1, s_res = sem("stats1"), sem("y1_done"), sem("res_done")
        s_rs1, s_rs2 = sem("deviation1"), sem("deviation2")
        s_xt, s_ct = sem("y1_transposed"), sem("ctx_transposed")
        s_xh, s_xl, s_ch, s_cl = sem("y1T_hi"), sem("y1T_lo"), sem("cT_hi"), sem("cT_lo")
        s_q, s_k, s_v = sem("q_product"), sem("k_product"), sem("v_product")
        s_qh, s_ql, s_kh, s_kl = sem("q_hi"), sem("q_lo"), sem("k_hi"), sem("k_lo")
        s_vh, s_vl = sem("v_hi"), sem("v_lo")
        n_st, n_v2 = sem("stacked"), sem("v_shifted")
        n_mr = [sem("max_rows_first"), sem("max_rows_second")]
        s_sc, s_mx = sem("scores"), sem("maxima")
        s_mt, s_mh, s_ml = sem("max_transposed"), sem("max_hi"), sem("max_lo")
        s_st, s_ph, s_pf = sem("scores_t"), sem("probs_hi"), sem("probs")
        s_pl = [sem("probs_lo_pool"), sem("probs_lo_vector")]
        s_av, s_a = sem("av_product"), sem("att_done")
        s_at, s_ah, s_al = sem("att_transposed"), sem("attT_hi"), sem("attT_lo")
        s_wo, s_x1 = sem("wo_product"), sem("x1_done")
        s_mv2, s_y2 = sem("stats2"), sem("y2_done")
        s_yt, s_yh, s_yl = sem("y2_transposed"), sem("y2T_hi"), sem("y2T_lo")
        s_lg, s_ls, s_ex, s_geq, s_cmp = (
            sem("logits"), sem("logits_less_max"), sem("gate_exp"), sem("experts_equal"), sem("experts_compared"))
        s_g, s_gT, s_gc = sem("gates_done"), sem("gates_transposed"), sem("gatesT_copied")
        s_b, s_ac = sem("bias_product"), sem("acc_started")
        s_mo = sem("expert_product")
        s_ma = sem("bank_read")
        s_fin, n_out = sem("out_final"), sem("stored")
        s_add = sem("vector_added")
        c_st1, c_st2, s_rd = sem("vector_stats1"), sem("vector_stats2"), sem("vector_denominators")
        c_gate = sem("vector_gate_chain")
        c_ln1, c_ln2, c_cmp, c_fin = sem("pool_norm1"), sem("pool_norm2"), sem("pool_compare"), sem("pool_final")

        def after(eng, s, value):
            if not (isinstance(value, int) and value <= 0):
                eng.wait_ge(s, value)

        tmp = e_in[:, :, :, :].rearrange("p (u b) q d -> p u b (q d)", u=2)

        def tok(t, i):
            return t.rearrange("b (c p) d -> b p c d", p=P)[i]

        def window(h, b):
            at = (2 * h + b % 2) * KW + b * BLK
            return k_op[:, at:at + 2 * BLK]

        def key_rows(copy, r, role, at):
            blocks = k_op[:, :].rearrange("p (h r b k) -> p h r b k", h=H, r=2, k=BLK)[:, :, r, at::2, :]
            copy(blocks, tmpl_k[:, role, :].unsqueeze(1).unsqueeze(1).to_broadcast(
                [P, H, len(range(at, NB + 1, 2)), BLK])).then_inc(s_kop, 1)

        def head_at(place):
            return place % KC * HH + place // KC

        def q_block(h, b):
            return q_op[:, h % HH * KC + h // HH, b * BLK:(b + 1) * BLK]

        WK, WQ, WV, WO = range(4)
        FIRST_BANKS = (4, 5, 6, 7)
        MAX_BANKS = (2, 7)
        FIRST_MAXIMA = 2
        LAST_BANKS = (0, 1, 4, 5, 6, 7)

        def expert_bank(j, t, e):
            return LAST_BANKS[(NEB * t + e) % len(LAST_BANKS)] if isinstance(j, int) and j == B - 1 else e % 2

        PASSES = [(0, 0), (0, 1), (1, 0)]
        NPREP = 4 + KC * NEB + 1

        def prep_bank(n):
            return n if n < 4 else 0 if n == 4 else n % 2

        IDENT_MADE, KEYS_MADE, QUERIES_MADE, POOL_CONSTS = 2, 9, 11, 17
        STACKED = 1 + 3 * KC + 3

        block = stack.enter_context(nc.Block())

        @block.sync
        def _(sp):
            def load_stacked(n, w):
                for k in range(KC):
                    sp.dma_start(w_in[:, n, k, :], w[k * P:(k + 1) * P, :].rearrange("(h d) i -> d h i", d=DK)).then_inc(n_w[n], 16)

            sp.dma_start(c_in[:], tok(ctx_in, 0)).then_inc(n_ctx, 16)
            load_stacked(WK, Wk)
            sp.dma_start(x_in[:], tok(x, 0)).then_inc(n_x, 16)
            load_stacked(WQ, Wq)
            for n, w in ((WV, Wv), (WO, Wo)):
                sp.dma_start(w_in[:, n, :, :], w.rearrange("(k p) i -> p k i", p=P)).then_inc(n_w[n], 16)
            for dst, src, w in ((g_in[:, 0:1], g_xattn, 1), (g_in[:, 1:2], g_ffn, 1), (bo_b[:, :], bo, D), (gb_b[:, :], gate_b, E)):
                sp.dma_start(dst, src.rearrange("(a b) -> a b", a=1).to_broadcast([P, w])).then_inc(n_s, 16)
            sp.dma_start(eb_in[:, :], expert_b).then_inc(n_s, 16)
            sp.dma_start(gw_in[:], gate_w).then_inc(n_gw, 16)
            sp.dma_start(e_in[:], expert_w.rearrange("e (k p) i -> p e k i", p=P)).then_inc(n_e, 16)

            def load_next(i):
                sp.wait_ge(s_res, i + 1)
                sp.dma_start(x_in[:], tok(x, i + 1)).then_inc(n_x, 16)
                sp.wait_ge(s_ct, KC * (i + 1))
                sp.dma_start(c_in[:], tok(ctx_in, i + 1)).then_inc(n_ctx, 16)

            def stack_q(i):
                for done, rows in ((s_qh, ((0, 0), (1, 0))), (s_ql, ((2, 1),))):
                    sp.wait_ge(done, KC * (i + 1))
                    for r, part in rows:
                        sp.dma_start(q_op[r * DK:(r + 1) * DK, :, :], qs[:, part, :, :]).then_inc(n_st, 16)

            def stack_k(i):
                after(sp, s_st, 2 * TP * i)
                if isinstance(i, int) and i == 0:
                    sp.wait_ge(s_zr, 1)
                    sp.wait_ge(s_kop, 5)
                    sp.wait_ge(s_qop, 1)
                sp.dma_start(q_op[3 * DK:3 * DK + 2, :, :], zrow[:, :]).then_inc(n_st, 16)
                for j in range(KC):
                    for done, rows in ((s_kh, ((0, 0), (2, 0))), (s_kl, ((1, 1),))):
                        sp.wait_ge(done, KC * i + j + 1)
                        for r, part in rows:
                            to = k_op[r * DK:(r + 1) * DK, :].rearrange("p (r c) -> p r c", c=KW)
                            sp.dma_start(to[:, 2 * HH * j:2 * HH * (j + 1), BLK:KW],
                                         ks[:, part, j, :].unsqueeze(1).to_broadcast([P, 2, S])).then_inc(n_st, 16)

            def shift_v(i):
                sp.wait_ge(s_vl, 2 * (i + 1))
                sp.dma_start(vv[BLK:P, :, 0, :, :, :], vv[0:BLK, :, 1, :, :, :]).then_inc(n_v2, 16)
                sp.dma_start(vv[0:BLK, :, 0, 1:TP, :, :], vv[BLK:P, :, 1, 0:TP - 1, :, :]).then_inc(n_v2, 16)

            def max_rows(i, half):
                sp.wait_ge(s_ml, 2 * i + half + 1)
                cols = slice(half * 2 * P, (half + 1) * 2 * P)
                for part in range(2):
                    r = 3 * DK + part
                    sp.dma_start(q_op[r:r + 1, :, cols], mxT[:, part, cols]).then_inc(n_mr[half], 16)

            def store(j, t, last=False):
                if t == 2 or last and t == 3:
                    sp.wait_ge(s_add, E * (j + 1) + E * (t - 2))
                else:
                    sp.wait_ge(s_fin, 3 * j + (3, 4, 0, 5)[t])
                sp.dma_start(tok(out, j)[:, t, :], acc[:, t, :]).then_inc(n_out, 16)

            def batch(i, experts, more):
                max_rows(i, 0)
                if more:
                    load_next(i)
                max_rows(i, 1)
                if experts:
                    store(i - 1, 0)
                    store(i - 1, 1)
                if more:
                    stack_k(i + 1)
                    stack_q(i + 1)
                if experts:
                    store(i - 1, 2)
                if more:
                    shift_v(i + 1)
                if experts:
                    store(i - 1, 3)

            stack_k(0)
            stack_q(0)
            shift_v(0)
            sp.wait_ge(s_ebl, 1)
            for r, part in enumerate((0, 1, 0)):
                sp.dma_start(eb3[r * E:(r + 1) * E, :], ebp[:, part, :]).then_inc(n_eb3, 16)
            batch(0, False, True)
            with sp.Fori(1, B - 1) as i:
                batch(i, True, True)
            batch(B - 1, True, False)
            for t in range(TP):
                store(B - 1, t, last=True)
            sp.wait_ge(n_out, 16 * TP * B + 16)

        @block.tensor
        def _(pe):
            def prep(n):
                if n < 4:
                    pe.wait_ge(n_w[n], 32 if n in (WK, WQ) else 16)
                    ins = [(k * D + o * P, w_in[:, n, o, k * P:(k + 1) * P]) for k in range(KC) for o in range(KC)]
                elif n == 4:
                    pe.wait_ge(n_gw, 16)
                    pe.wait_ge(s_wl, 1)
                    ins = [(k * E, gw_in[:, k * P:(k + 1) * P]) for k in range(KC)]
                else:
                    pe.wait_ge(n_e, 16)
                    if n == 5:
                        pe.wait_ge(s_bo, 1)
                    else:
                        pe.wait_ge(s_wl, max(n - 1, 5))
                    eb, k = divmod(n - 5, KC)
                    ins = [(q * P, e_in[:, 2 * eb + q // 2, q % 2, k * P:(k + 1) * P]) for q in range(4)]
                for col, src in ins:
                    r, w = src.shape
                    mm = pe.transpose(ps[0:w, prep_bank(n), col:col + r], src, ident[0:r, 0:r])
                mm.then_inc(s_wt, 1)

            def transpose(bank, src, k, done):
                for t in range(TP):
                    mm = pe.transpose(ps[:, bank, t * P:(t + 1) * P], src[:, t, k * P:(k + 1) * P], ident[:, :])
                mm.then_inc(done, 1)

            def y1_transposes(i, k):
                pe.wait_ge(s_y1, TP * (i + 1))
                transpose(6 + k, y1, k, s_xt)

            def ctx_transposes(i, k):
                pe.wait_ge(n_ctx, 16 * (i + 1))
                transpose(4 + k, c_in, k, s_ct)

            def project(bank, w, src, j, done):
                n = 0
                for k in range(KC):
                    for a, b in PASSES:
                        mm = pe.matmul(ps[:, bank + j, :], wT[:, b, w, k, j * P:(j + 1) * P], src[:, a, k, :],
                                       start=n == 0, stop=n == 5)
                        n += 1
                mm.then_inc(done, 1)

            def project_k(i):
                pe.wait_ge(s_cl, KC * (i + 1))
                for j in range(KC):
                    project(4, WK, cT, j, s_k)

            def project_q(i):
                pe.wait_ge(s_xl, KC * (i + 1))
                for j in range(KC):
                    project(6, WQ, y1T, j, s_q)

            def by_token(bank, src, w, done, tiles=range(TP)):
                for t in tiles:
                    n = 0
                    for k in range(KC):
                        for a, b in PASSES:
                            mm = pe.matmul(ps[:, bank + t // 2, (t % 2) * D:(t % 2 + 1) * D],
                                           src[:, a, k, t * P:(t + 1) * P], wT[:, b, w, k, :],
                                           start=n == 0, stop=n == 5)
                            n += 1
                    if t % 2:
                        mm.then_inc(done, 1)

            def project_v(i, half):
                if half == 0:
                    pe.wait_ge(s_ql, KC * (i + 1))
                by_token(6, cT, WV, s_v, range(2 * half, 2 * half + 2))

            def gates_transposed(j):
                pe.wait_ge(s_g, j + 1)
                for t in range(TP):
                    mm = pe.transpose(ps[0:3 * E, 2, :].bitcast(F16)[:, t * P:(t + 1) * P], g3[:, t, :], ident16[:, :])
                mm.then_inc(s_gT, 1)

            def gate_bias(j):
                pe.wait_ge(s_gc, j + 1)
                for t in range(TP):
                    mm = pe.matmul(ps[:, 3 - t // 2, (t % 2) * D:(t % 2 + 1) * D], g3T[:, t * P:(t + 1) * P], eb3[:, :],
                                   start=True, stop=True)
                    if t % 2:
                        mm.then_inc(s_b, 1)

            def experts(j, t, e):
                if t == 2 and e >= 2:
                    pe.wait_ge(s_add, E * j + 2 * (e - 1))
                elif t == 3 and e < 2:
                    pe.wait_ge(s_add, E * j + 2 * (e + 3))
                else:
                    pe.wait_ge(s_ma, 3 * NEB * j + NEB * min(t, 2) + e + 1)
                if t == 0 and e == 0:
                    pe.wait_ge(s_ls, j + 1)
                expert_product(t, e, e % 2)

            def last_experts(n):
                j = B - 1
                t, e = divmod(n, NEB)
                back = n - len(LAST_BANKS)
                if n < 2:
                    pe.wait_ge(s_ma, 3 * NEB * j + n + 1)
                elif back >= 2 * NEB:
                    pe.wait_ge(s_add, E * j + 2 * (back - 2 * NEB + 1))
                elif back >= 0:
                    pe.wait_ge(s_ma, 3 * NEB * j + back + 3)
                if n == 0:
                    pe.wait_ge(s_ls, j + 1)
                expert_product(t, e, LAST_BANKS[n % len(LAST_BANKS)])

            def expert_product(t, e, bank):
                m = 0
                for k in range(KC):
                    for a, w in PASSES:
                        mm = pe.matmul(ps[:, bank, :], y2T[:, a, k, t * P:(t + 1) * P],
                                       eT[:, w, k, e * 512:(e + 1) * 512], start=m == 0, stop=m == 5)
                        m += 1
                mm.then_inc(s_mo, 1)

            def first_pass(i, g):
                c, hq = divmod(g, 4)
                bank = FIRST_BANKS[g % 4]
                if g == 0:
                    pe.wait_ge(n_st, 16 * STACKED * (i + 1))
                if g in (2, 3):
                    pe.wait_ge(s_vl, 2 * i + g - 1)
                if g >= 4:
                    pe.wait_ge(s_mx, 4 * TP * i + g - 3)
                for hh in range(4):
                    for par in range(2):
                        h, b = head_at(4 * hq + hh), 2 * c + par
                        mm = pe.matmul(ps[BLK * par:BLK * (par + 1), bank, hh * P:(hh + 1) * P],
                                       q_block(h, b), window(h, b), start=True, stop=True)
                mm.then_inc(s_sc, 1)

            def max_transposes(i, half):
                pe.wait_ge(s_mx, 4 * TP * i + 2 * TP * (half + 1))
                if half == 0:
                    after(pe, s_ac, 2 * i)
                for t in range(2 * half, 2 * half + 2):
                    mm = pe.transpose(ps[0:H, MAX_BANKS[half], t * P:(t + 1) * P], mx[:, t, :], ident[:, :])
                mm.then_inc(s_mt, 1)

            def second_pass(i, u):
                c, half = divmod(u, 2)
                if u % TP == 0:
                    pe.wait_ge(n_mr[u // TP], 32 * (i + 1))
                if u >= 2:
                    pe.wait_ge(s_pf, 2 * TP * i + u - 1)
                for hh in range(HH):
                    for par in range(2):
                        h, b = HH * half + hh, 2 * c + par
                        col = (2 * hh + par) * BLK
                        mm = pe.matmul(ps[:, 2 + 2 * (u % 2) + col // 512, col % 512:col % 512 + BLK],
                                       window(h, b), q_block(h, b), start=True, stop=True)
                mm.then_inc(s_st, 1)

            def values(i, u):
                c, half = divmod(u, 2)
                pe.wait_ge(s_pl[u % 2], TP * i + u // 2 + 1)
                if u == 0:
                    pe.wait_ge(n_v2, 32 * (i + 1))
                if u == 1:
                    pe.wait_ge(s_ml, 2 * (i + 1))
                if u >= 2:
                    pe.wait_ge(s_a, 2 * TP * i + u - 1)
                for hh in range(HH):
                    for n, (a, b) in enumerate(PASSES):
                        mm = pe.matmul(ps[:, 6 + half, hh * 2 * V1:(hh + 1) * 2 * V1],
                                       pr[:, u % 3, a, hh * P:(hh + 1) * P], vv[:, b, :, c, HH * half + hh, :],
                                       start=n == 0, stop=n == 2)
                mm.then_inc(s_av, 1)

            def output_projection(i):
                pe.wait_ge(s_al, KC * (i + 1))
                by_token(2, attT, WO, s_wo)

            def gate_logits(i, with_experts):
                pe.wait_ge(s_yl, KC * (i + 1))
                if with_experts:
                    pe.wait_ge(s_ma, 3 * NEB * i + 1)
                else:
                    pe.wait_ge(s_wl, NPREP)
                for t in range(TP):
                    n = 0
                    for k in range(KC):
                        for a, w in PASSES:
                            mm = pe.matmul(ps[:, 0, t * E:(t + 1) * E], y2T[:, a, k, t * P:(t + 1) * P],
                                           gwT[:, w, k, :], start=n == 0, stop=n == 5)
                            n += 1
                mm.then_inc(s_lg, 1)

            def batch(i, with_experts, more):
                def expert(t, e):
                    if with_experts:
                        experts(i - 1, t, e)

                if not with_experts:
                    for g in range(3):
                        first_pass(i, g)
                expert(0, 0)
                first_pass(i, 3)
                expert(0, 1)
                for g in range(4, 4 * TP):
                    first_pass(i, g)
                    if not with_experts and g in (12, 14):
                        prep(g // 2 - 1)
                    if g == 4 and with_experts:
                        gates_transposed(i - 1)
                    if g == 6 and with_experts:
                        gate_bias(i - 1)
                    if g == 8:
                        expert(0, 2)
                    if g == 11:
                        expert(0, 3)
                        max_transposes(i, 0)
                    if g == 13:
                        expert(1, 0)
                    if g == 15:
                        expert(1, 1)
                if not with_experts:
                    prep(7)
                    prep(8)
                max_transposes(i, 1)
                second_pass(i, 0)
                expert(1, 2)
                second_pass(i, 1)
                expert(1, 3)
                for u in range(2 * TP):
                    if u + 2 < 2 * TP:
                        second_pass(i, u + 2)
                    if u in (0, 1, 2, 4):
                        expert(2, (0, 1, 2, 4).index(u))
                    if u >= 6 and more:
                        expert(3, u - 6)
                    values(i, u)
                if more:
                    for k in range(KC):
                        ctx_transposes(i + 1, k)
                pe.wait_ge(s_a, 2 * TP * (i + 1))
                for k in range(KC):
                    transpose(2 + k, att, k, s_at)
                if more:
                    expert(3, 2)
                    for k in range(KC):
                        y1_transposes(i + 1, k)
                else:
                    expert(3, 0)
                output_projection(i)
                if not more:
                    expert(3, 1)
                    expert(3, 2)
                if more:
                    project_k(i + 1)
                    project_q(i + 1)
                expert(3, 3)
                if not with_experts:
                    for n in range(9, NPREP):
                        prep(n)
                pe.wait_ge(s_y2, TP * (i + 1))
                for k in range(KC):
                    transpose(2 + k, y2, k, s_yt)
                if more:
                    project_v(i + 1, 0)
                gate_logits(i, with_experts)
                if more:
                    project_v(i + 1, 1)
                    for g in range(3):
                        first_pass(i + 1, g)

            pe.wait_ge(s_pc, IDENT_MADE)
            for k in range(KC):
                ctx_transposes(0, k)
            prep(WK)
            prep(WQ)
            for k in range(KC):
                y1_transposes(0, k)
            pe.wait_ge(s_wl, WK + 1)
            project_k(0)
            pe.wait_ge(s_wl, WQ + 1)
            project_q(0)
            prep(WV)
            prep(WO)
            prep(4)
            pe.wait_ge(s_wl, WV + 1)
            for half in range(2):
                project_v(0, half)
            pe.wait_ge(s_wl, WO + 1)
            pe.wait_ge(s_bl, 1)
            n = 0
            for k in range(KC):
                for a, b in PASSES:
                    mm = pe.matmul(ps[:, 1, 0:D], bv_p[:, a, k, :], wT[:, b, WO, k, :], start=n == 0, stop=n == 5)
                    n += 1
            mm.then_inc(s_bp, 1)
            batch(0, False, True)
            pe.wait_ge(s_pc, POOL_CONSTS)
            pe.wait_ge(n_eb3, 48)
            with pe.Fori(1, B - 1) as i:
                batch(i, True, True)
            batch(B - 1, True, False)
            for n in range(TP * NEB):
                last_experts(n)
                if n == 3:
                    gates_transposed(B - 1)
                if n == 4:
                    gate_bias(B - 1)

        @block.scalar
        def _(act):
            def high(dst, src, ready, count, done, scale=1.0, bias=0.0):
                act.wait_ge(ready, count)
                act.activation(dst, src, ACT.Identity, scale=scale, bias=bias).then_inc(done, 1)

            with nc.allow_non_contiguous_dma(reason="256 biases into their partitions, once"):
                for n, src in ((1, bk), (0, bq)):
                    for j in range(KC):
                        act.dma_start(qkb[:, n, j:j + 1],
                                      src[j * P:(j + 1) * P].rearrange("(h d a) -> d h a", d=DK, a=1)).then_inc(n_c, 16)
                act.dma_start(bv_c[:, :], bv.rearrange("(k p) -> p k", p=P)).then_inc(n_c, 16)

            def prep_high(n):
                if n < 4:
                    high(wT[:, 0, n, :, :].rearrange("p k o -> p (k o)"), ps[:, prep_bank(n), :], s_wt, n + 1, s_wh,
                         scale=QS if n == WQ else WS)
                elif n == 4:
                    high(gwT[:, 0, :, :].rearrange("p k o -> p (k o)"), ps[:, 0, 0:KC * E], s_wt, n + 1, s_wh, scale=WS)
                else:
                    eb, k = divmod(n - 5, KC)
                    high(eT[:, 0, k, eb * 512:(eb + 1) * 512], ps[:, prep_bank(n), :], s_wt, n + 1, s_wh, scale=WS)

            def y1_high(i):
                for k in range(KC):
                    high(y1T[:, 0, k, :], ps[:, 6 + k, :], s_xt, KC * i + k + 1, s_xh)

            def ctx_high(i):
                for k in range(KC):
                    high(cT[:, 0, k, :], ps[:, 4 + k, :], s_ct, KC * i + k + 1, s_ch)

            def experts(j, t, e):
                act.wait_ge(s_mo, TP * NEB * j + NEB * t + e + 1)
                if e == 0:
                    if t == 0:
                        act.wait_ge(s_g, j + 1)
                    act.wait_ge(s_fin, 3 * j + (2, 1, 0, 3)[t])
                for q in range(2):
                    a = act.activation(tmp[:, t % 3 % 2, e, q * D:(q + 1) * D], ps[:, expert_bank(j, t, e), q * D:(q + 1) * D], ACT.Copy,
                                       scale=gs[:, t, 2 * e + q:2 * e + q + 1])
                a.then_inc(s_ma, 1)

            def k_high(i):
                after(act, n_st, 16 * STACKED * i)
                for j in range(KC):
                    high(ks[:, 0, j, :], ps[:, 4 + j, :], s_k, KC * i + j + 1, s_kh, bias=qkbs[:, 1, j:j + 1])

            def q_high(i):
                for j in range(KC):
                    high(qs[:, 0, j, :], ps[:, 6 + j, :], s_q, KC * i + j + 1, s_qh, bias=qkbs[:, 0, j:j + 1])

            def v_high(i, q):
                if q == 0:
                    after(act, s_av, 2 * TP * i)
                high(vv[:, 0, 1, 2 * q:2 * q + 2, :, 0:DK], ps[:, 6 + q, :].rearrange("p (t h d) -> p t h d", t=2, h=H),
                     s_v, 2 * i + q + 1, s_vh)

            def copy_gates(j):
                act.wait_ge(s_gT, j + 1)
                act.activation(g3T[:, :], ps[0:3 * E, 2, :].bitcast(F16)[:, 0:S], ACT.Copy).then_inc(s_gc, 1)

            def max_high(i, half):
                cols = slice(half * 2 * P, (half + 1) * 2 * P)
                high(mxT[:, 0, cols], ps[0:H, MAX_BANKS[half], cols], s_mt, 2 * i + half + 1, s_mh, scale=1.0 / SC)

            def exponentials(i, u):
                act.wait_ge(s_st, 2 * TP * i + u + 1)
                if u >= 3:
                    act.wait_ge(s_av, 2 * TP * i + u - 2)
                src = ps[:, 2 + 2 * (u % 2):4 + 2 * (u % 2), :].rearrange("p b c -> p (b c)")
                act.activation(pr[:, u % 3, 0, :], src, ACT.Exp, scale=1.0 / SC).then_inc(s_ph, 1)
                if u >= 2:
                    act.wait_ge(s_pl[u % 2], TP * i + u // 2)
                act.activation(pf[:, u % 2, :], src, ACT.Exp, scale=1.0 / SC).then_inc(s_pf, 1)

            def batch(i, with_experts, more):
                def expert(t, e):
                    if with_experts:
                        experts(i - 1, t, e)

                if with_experts:
                    copy_gates(i - 1)
                for e in range(4):
                    expert(0, e)
                max_high(i, 0)
                expert(1, 0)
                expert(1, 1)
                if not with_experts:
                    for n in range(5, 9):
                        prep_high(n)
                max_high(i, 1)
                exponentials(i, 0)
                expert(1, 2)
                exponentials(i, 1)
                expert(1, 3)
                for u in range(2, 2 * TP):
                    exponentials(i, u)
                if more:
                    expert(3, 0)
                    expert(3, 1)
                for k in range(KC):
                    high(attT[:, 0, k, :], ps[:, 2 + k, :], s_at, KC * i + k + 1, s_ah)
                if more:
                    ctx_high(i + 1)
                else:
                    expert(3, 0)
                    expert(3, 1)
                expert(3, 2)
                if more:
                    y1_high(i + 1)
                    k_high(i + 1)
                    q_high(i + 1)
                if not with_experts:
                    for n in range(9, NPREP):
                        prep_high(n)
                for k in range(KC):
                    high(y2T[:, 0, k, :], ps[:, 2 + k, :], s_yt, KC * i + k + 1, s_yh)
                expert(3, 3)
                if more:
                    v_high(i + 1, 0)
                act.wait_ge(s_ls, i + 1)
                act.activation(ex[:, :, :], ls[:, :, :], ACT.Exp).then_inc(s_ex, 1)
                if more:
                    v_high(i + 1, 1)

            ctx_high(0)
            prep_high(WK)
            prep_high(WQ)
            act.wait_ge(s_pc, KEYS_MADE)
            key_rows(lambda to, rows: act.activation(to, rows, ACT.Copy), 1, 1, 0)
            y1_high(0)
            act.wait_ge(s_sb, 2)
            k_high(0)
            q_high(0)
            for n in (WV, WO, 4):
                prep_high(n)
            act.wait_ge(s_bw, 1)
            act.activation(bv_p[:, 0, :, :], bv_w[:, :, :], ACT.Identity).then_inc(s_bh, 1)
            for q in range(2):
                v_high(0, q)
            act.wait_ge(n_s, 80)
            act.activation(tg[:, 0:2], g_in[:, :], ACT.Tanh).then_inc(s_tg, 1)
            act.activation(ebp[:, 0, :], eb_in[:, :], ACT.Identity).then_inc(s_ebh, 1)
            batch(0, False, True)
            with act.Fori(1, B - 1) as i:
                batch(i, True, True)
            batch(B - 1, True, False)
            copy_gates(B - 1)
            for t in range(2):
                for e in range(NEB):
                    experts(B - 1, t, e)

        @block.vector
        def _(dve):
            class Chain:
                def __init__(self, s, per):
                    self.s, self.per, self.n = s, per, 0

                def begin(self, i):
                    self.i, self.n = i, 0

                def link(self, ins):
                    ins.then_inc(self.s, 1)
                    self.n += 1
                    dve.wait_ge(self.s, self.i * self.per + self.n)

                def end(self):
                    assert self.n == self.per, (self.n, self.per)

            gate_chain = Chain(c_gate, 8)

            def low(dst, src, hi, ready, count, done, scale=1.0, bias=None):
                dve.wait_ge(ready, count)
                if bias is not None:
                    dve.scalar_tensor_tensor(dst, src, bias, hi, ALU.add, ALU.subtract).then_inc(done, 1)
                elif scale != 1.0:
                    dve.scalar_tensor_tensor(dst, src, scale, hi, ALU.mult, ALU.subtract).then_inc(done, 1)
                else:
                    dve.tensor_tensor(dst, src, hi, ALU.subtract).then_inc(done, 1)

            def prep_low(n):
                if n < 4:
                    low(wT[:, 1, n, :, :].rearrange("p k o -> p (k o)"), ps[:, prep_bank(n), :],
                        wT[:, 0, n, :, :].rearrange("p k o -> p (k o)"), s_wh, n + 1, s_wl, scale=QS if n == WQ else WS)
                elif n == 4:
                    low(gwT[:, 1, :, :].rearrange("p k o -> p (k o)"), ps[:, 0, 0:KC * E],
                        gwT[:, 0, :, :].rearrange("p k o -> p (k o)"), s_wh, n + 1, s_wl, scale=WS)
                else:
                    eb, k = divmod(n - 5, KC)
                    low(eT[:, 1, k, eb * 512:(eb + 1) * 512], ps[:, prep_bank(n), :],
                        eT[:, 0, k, eb * 512:(eb + 1) * 512], s_wh, n + 1, s_wl, scale=WS)

            def norm_statistics(i):
                dve.wait_ge(n_x, 16 * (i + 1))
                for t in range(TP):
                    a = dve.bn_stats(st1[:, t, :], x_in[:, t, :])
                a.then_inc(c_st1, 1)
                dve.wait_ge(s_pc, 1)
                dve.wait_ge(c_st1, i + 1)
                for t in range(TP):
                    a = dve.bn_aggr(mv1[:, t, :], st1[:, t, :])
                a.then_inc(s_mv1, 1)

            def normalise(src, mv, rs, dst, done):
                for t in range(TP):
                    dve.tensor_scalar(dst[:, t, :], src[:, t, :], mv[:, t, 0:1], rs[:, t:t + 1],
                                      ALU.subtract, ALU.mult).then_inc(done, 1)

            def first_norm(i):
                after(dve, s_xt, KC * i)
                dve.wait_ge(s_rs1, i + 1)
                normalise(x_in, mv1, rs1, y1, s_y1)

            def second_norm(i):
                after(dve, s_yt, KC * i)
                dve.wait_ge(s_rs2, i + 1)
                normalise(res, mv2, rs2, y2, s_y2)

            def second_statistics(i, q):
                dve.wait_ge(s_x1, 2 * i + q + 1)
                for t in range(2 * q, 2 * q + 2):
                    a = dve.bn_stats(st2[:, t, :], res[:, t, :])
                if q == 1:
                    a.then_inc(c_st2, 1)

            def second_aggregate(i):
                dve.wait_ge(s_pc, 1)
                dve.wait_ge(c_st2, i + 1)
                for t in range(TP):
                    a = dve.bn_aggr(mv2[:, t, :], st2[:, t, :])
                a.then_inc(s_mv2, 1)

            def y1_low(i):
                for k in range(KC):
                    low(y1T[:, 1, k, :], ps[:, 6 + k, :], y1T[:, 0, k, :], s_xh, KC * i + k + 1, s_xl)

            def ctx_low(i):
                for k in range(KC):
                    low(cT[:, 1, k, :], ps[:, 4 + k, :], cT[:, 0, k, :], s_ch, KC * i + k + 1, s_cl)

            def maximum(i, g):
                c, hq = divmod(g, 4)
                dve.wait_ge(s_sc, 4 * TP * i + g + 1)
                dve.tensor_reduce(mx[:, c, 4 * hq:4 * hq + 4], ps[:, FIRST_BANKS[g % 4], :].rearrange("p (h k) -> p h k", h=4),
                                  AX.X, ALU.max).then_inc(s_mx, 1)

            def gates(i, more):
                gate_chain.begin(i)
                link = gate_chain.link
                dve.wait_ge(s_lg, i + 1)
                link(dve.scalar_tensor_tensor(lg[:, :, :], ps[:, 0, 0:TP * E].rearrange("p (t e) -> p t e", e=E), 1.0 / WS,
                                              gb_b[:, :].unsqueeze(1).to_broadcast([P, TP, E]), ALU.mult, ALU.add))
                link(dve.tensor_reduce(lmx[:, :], lg[:, :, :], AX.X, ALU.max))
                dve.tensor_tensor(ls[:, :, :], lg[:, :, :], lmx[:, :].unsqueeze(2).to_broadcast([P, TP, E]),
                                  ALU.subtract).then_inc(s_ls, 1)
                dve.wait_ge(s_ex, i + 1)
                mine = ex[:, :, :].unsqueeze(3).to_broadcast([P, TP, E, E])
                other = ex[:, :, :].unsqueeze(2).to_broadcast([P, TP, E, E])
                dve.tensor_tensor(gtw[:, :, :, :], other, mine, ALU.is_gt)
                dve.tensor_tensor(geq[:, :, :, :], other, mine, ALU.is_equal).then_inc(s_geq, 1)
                link(dve.tensor_reduce(esum[:, :], ex[:, :, :], AX.X, ALU.add))
                link(dve.reciprocal(erec[:, :], esum[:, :]))
                if more:
                    v_low(i + 1, 1)
                    for g in range(FIRST_MAXIMA):
                        maximum(i + 1, g)
                dve.wait_ge(s_cmp, i + 1)
                link(dve.tensor_reduce(rank[:, :, :], gtw[:, :, :, :], AX.X, ALU.add))
                link(dve.scalar_tensor_tensor(gsel[:, :, :], rank[:, :, :], 1.5, ex[:, :, :], ALU.is_lt, ALU.mult))
                link(dve.scalar_tensor_tensor(gt[:, :, :], gsel[:, :, :], tg[:, 1:2],
                                              erec[:, :].unsqueeze(2).to_broadcast([P, TP, E]), ALU.mult, ALU.mult))
                dve.tensor_scalar(gs[:, :, :], gt[:, :, :], 1.0 / WS, None, ALU.mult)
                dve.tensor_copy(g3[:, :, 0:E], gt[:, :, :])
                link(dve.tensor_copy(g3[:, :, E:2 * E], gt[:, :, :]))
                dve.tensor_tensor(g3[:, :, 2 * E:3 * E], gt[:, :, :], g3[:, :, 0:E], ALU.subtract).then_inc(s_g, 1)
                gate_chain.end()

            def start_acc(j):
                dve.wait_ge(n_out, 16 * TP * j + 16)
                for q in range(2):
                    dve.wait_ge(s_b, 2 * j + q + 1)
                    dve.tensor_tensor(acc[:, 2 * q:2 * q + 2, :].rearrange("p t d -> p (t d)"), ps[:, 3 - q, :],
                                      res[:, 2 * q:2 * q + 2, :].rearrange("p t d -> p (t d)"), ALU.add).then_inc(s_ac, 1)

            def q_low(i):
                for j in range(KC):
                    low(qs[:, 1, j, :], ps[:, 6 + j, :], qs[:, 0, j, :], s_qh, KC * i + j + 1, s_ql,
                        bias=qkbs[:, 0, j:j + 1])

            def k_low(i):
                for j in range(KC):
                    low(ks[:, 1, j, :], ps[:, 4 + j, :], ks[:, 0, j, :], s_kh, KC * i + j + 1, s_kl,
                        bias=qkbs[:, 1, j:j + 1])

            def v_low(i, q):
                low(vv[:, 1, 1, 2 * q:2 * q + 2, :, 0:DK], ps[:, 6 + q, :].rearrange("p (t h d) -> p t h d", t=2, h=H),
                    vv[:, 0, 1, 2 * q:2 * q + 2, :, 0:DK], s_vh, 2 * i + q + 1, s_vl)

            def normalise_att(i, u):
                c, half = divmod(u, 2)
                o = ps[:, 6 + half, 0:HH * 2 * V1].rearrange("p (h r v) -> p h r v", h=HH, r=2)
                dve.wait_ge(s_av, 2 * TP * i + u + 1)
                dve.reciprocal(rden[:, half, :], o[:, :, 1, DK]).then_inc(s_rd, 1)
                dve.wait_ge(s_rd, 2 * TP * i + u + 1)
                for r in range(2):
                    rows = slice(r * BLK, (r + 1) * BLK)
                    a = dve.tensor_tensor(
                        att[rows, c, half * P:(half + 1) * P].rearrange("p (h d) -> p h d", h=HH),
                        o[rows, :, r, 0:DK],
                        rden[rows, half, :].unsqueeze(2).to_broadcast([BLK, HH, DK]), ALU.mult)
                a.then_inc(s_a, 1)

            def max_low(i, half):
                cols = slice(half * 2 * P, (half + 1) * 2 * P)
                low(mxT[:, 1, cols], ps[0:H, MAX_BANKS[half], cols], mxT[:, 0, cols], s_mh, 2 * i + half + 1, s_ml,
                    scale=1.0 / SC)

            def probs_low(i, u):
                if u >= 3:
                    dve.wait_ge(s_av, 2 * TP * i + u - 2)
                low(pr[:, u % 3, 1, :], pf[:, 1, :], pr[:, u % 3, 0, :], s_pf, 2 * TP * i + u + 1, s_pl[1])

            def experts(j, t, e):
                first = E * j + E * (t - 2) + 2 * e
                dve.wait_ge(s_mo, TP * NEB * j + NEB * t + e + 1)
                for q in range(2):
                    if e + q:
                        dve.wait_ge(s_add, first + q)
                    else:
                        dve.wait_ge(s_ac, 2 * j + 2)
                    dve.scalar_tensor_tensor(acc[:, t, :], ps[:, expert_bank(j, t, e), q * D:(q + 1) * D],
                                             gs[:, t, 2 * e + q:2 * e + q + 1], acc[:, t, :],
                                             ALU.mult, ALU.add).then_inc(s_add, 1)

            def batch(i, with_experts, more):
                for g in range(FIRST_MAXIMA if with_experts else 0, 4 * TP):
                    maximum(i, g)
                    if with_experts and g == 7:
                        start_acc(i - 1)
                    if g == 11:
                        max_low(i, 0)
                    if not with_experts and g > 12:
                        prep_low(g - 8)
                if not with_experts:
                    prep_low(8)
                max_low(i, 1)
                for u in range(2 * TP):
                    if u % 2:
                        probs_low(i, u)
                    if u >= 1:
                        normalise_att(i, u - 1)
                    if more and u == 0:
                        norm_statistics(i + 1)
                    if with_experts and u in (1, 2, 4, 5):
                        experts(i - 1, 2, (1, 2, 4, 5).index(u))
                normalise_att(i, 2 * TP - 1)
                if more:
                    first_norm(i + 1)
                for k in range(KC):
                    low(attT[:, 1, k, :], ps[:, 2 + k, :], attT[:, 0, k, :], s_ah, KC * i + k + 1, s_al)
                if more:
                    ctx_low(i + 1)
                    y1_low(i + 1)
                dve.wait_ge(s_res, i + 1)
                for q in range(2):
                    dve.wait_ge(s_wo, 2 * i + q + 1)
                    r = res[:, 2 * q:2 * q + 2, :].rearrange("p t d -> p (t d)")
                    dve.scalar_tensor_tensor(r, ps[:, 2 + q, :], tg[:, 2:3], r, ALU.mult, ALU.add).then_inc(s_x1, 1)
                    second_statistics(i, q)
                second_aggregate(i)
                if more:
                    k_low(i + 1)
                second_norm(i)
                if more:
                    q_low(i + 1)
                if not with_experts:
                    for n in range(9, NPREP):
                        prep_low(n)
                for k in range(KC):
                    low(y2T[:, 1, k, :], ps[:, 2 + k, :], y2T[:, 0, k, :], s_yh, KC * i + k + 1, s_yl)
                if more:
                    v_low(i + 1, 0)
                gates(i, more)

            dve.memset(zrow[:, :], 0.0).then_inc(s_zr, 1)
            dve.memset(vv[:, 0, 1, :, :, DK:V1], WS)
            dve.memset(vv[:, 1, 1, :, :, DK:V1], 0.0)
            dve.memset(bv_w[:, :, :], 0.0).then_inc(s_bz, 1)
            dve.memset(vv[0:BLK, :, 0, 0, :, :], 0.0)
            dve.memset(acc[:, 0, 0:1], 0.0).then_inc(n_out, 16)

            dve.wait_ge(s_pc, KEYS_MADE)
            key_rows(dve.tensor_copy, 0, 0, 2)
            key_rows(dve.tensor_copy, 0, 1, 1)
            key_rows(dve.tensor_copy, 1, 0, 1)
            norm_statistics(0)
            ctx_low(0)
            first_norm(0)
            prep_low(WK)
            dve.wait_ge(n_c, 80)
            dve.tensor_scalar(qkbs[:, 1, :], qkb[:, 1, :], WS, None, ALU.mult).then_inc(s_sb, 1)
            dve.tensor_scalar(qkbs[:, 0, :], qkb[:, 0, :], QS, None, ALU.mult).then_inc(s_sb, 1)
            prep_low(WQ)
            dve.tensor_copy(k_op[:, :].rearrange("p (h c) -> p h c", h=H)[:, :, 0:BLK],
                            tmpl_k[:, 2, :].unsqueeze(1).to_broadcast([P, H, BLK])).then_inc(s_kop, 1)
            dve.wait_ge(s_pc, QUERIES_MADE)
            dve.tensor_copy(q_op[:, :, :].rearrange("p h (b q) -> p (h b) q", q=BLK),
                            tmpl_q[:, :].unsqueeze(1).to_broadcast([P, H * NB, BLK])).then_inc(s_qop, 1)
            y1_low(0)
            dve.wait_ge(s_sb, 2)
            k_low(0)
            q_low(0)
            dve.wait_ge(s_bz, 1)
            dve.tensor_tensor(bv_w[:, :, :], bv_w[:, :, :], bv_c[:, :].unsqueeze(2).to_broadcast([P, KC, P]),
                              ALU.add).then_inc(s_bw, 1)
            for n in (WV, WO, 4):
                prep_low(n)
            dve.wait_ge(s_bh, 1)
            dve.tensor_tensor(bv_p[:, 1, :, :], bv_w[:, :, :], bv_p[:, 0, :, :], ALU.subtract).then_inc(s_bl, 1)
            for q in range(2):
                v_low(0, q)
            dve.wait_ge(s_tg, 1)
            dve.tensor_scalar(tg[:, 2:3], tg[:, 0:1], 1.0 / WS, None, ALU.mult).then_inc(s_tgs, 1)
            dve.wait_ge(s_ebh, 1)
            dve.tensor_tensor(ebp[:, 1, :], eb_in[:, :], ebp[:, 0, :], ALU.subtract).then_inc(s_ebl, 1)
            dve.wait_ge(s_bp, 1)
            dve.scalar_tensor_tensor(bo_b[:, :], ps[:, 1, 0:D], 1.0 / WS, bo_b[:, :], ALU.mult, ALU.add).then_inc(s_bo, 1)
            dve.wait_ge(s_bo, 1)
            dve.tensor_scalar(bot[:, :], bo_b[:, :], tg[:, 0:1], None, ALU.mult).then_inc(s_bo, 1)
            dve.wait_ge(s_tgs, 1)
            batch(0, False, True)
            with dve.Fori(1, B - 1) as i:
                batch(i, True, True)
            batch(B - 1, True, False)
            start_acc(B - 1)
            for t in (2, 3):
                for e in range(NEB):
                    experts(B - 1, t, e)

        @block.gpsimd
        def _(pool):
            made = [0]

            def const(ins):
                ins.then_inc(s_pc, 1)
                made[0] += 1
                pool.wait_ge(s_pc, made[0])

            def identity(t):
                const(pool.memset(t[:, :], 0.0))
                const(pool.affine_select(out=t[:, :], in_=t[:, :], compare_op=ALU.not_equal, fill=1.0, base=0,
                                         pattern=[[-1, P]], channel_multiplier=1))

            identity(ident)
            assert made[0] == IDENT_MADE
            const(pool.memset(tmpl_k[:, :, :], 0.0))
            const(pool.affine_select(out=tmpl_k[:, 0, :], in_=tmpl_k[:, 0, :], compare_op=ALU.is_ge, fill=MASKED,
                                     base=BLK, pattern=[[1, BLK]], channel_multiplier=-1))
            const(pool.affine_select(out=tmpl_k[:, 1, :], in_=tmpl_k[:, 1, :], compare_op=ALU.is_ge, fill=MASKED,
                                     base=-BLK, pattern=[[-1, BLK]], channel_multiplier=1))
            const(pool.affine_select(out=tmpl_k[:, 1, :], in_=tmpl_k[:, 1, :], compare_op=ALU.is_ge, fill=0.0,
                                     base=-BLK, pattern=[[0, BLK]], channel_multiplier=1))
            const(pool.affine_select(out=tmpl_k[:, 2, :], in_=tmpl_k[:, 2, :], compare_op=ALU.is_ge, fill=MASKED,
                                     base=BLK - 1, pattern=[[0, BLK]], channel_multiplier=-1))
            for r in range(2):
                const(pool.affine_select(out=tmpl_k[:, :, :], in_=tmpl_k[:, :, :], compare_op=ALU.not_equal, fill=-SC,
                                         base=-(3 * DK + r), pattern=[[0, 3], [0, BLK]], channel_multiplier=1))
            assert made[0] == KEYS_MADE
            const(pool.memset(tmpl_q[:, :], 0.0))
            const(pool.affine_select(out=tmpl_q[:, :], in_=tmpl_q[:, :], compare_op=ALU.not_equal, fill=ONEHOT,
                                     base=-BLK, pattern=[[-1, BLK]], channel_multiplier=1))
            assert made[0] == QUERIES_MADE
            identity(ident16)
            const(pool.memset(lower[:, :, :], 1.0))
            const(pool.affine_select(out=lower[:, :, :], in_=lower[:, :, :], compare_op=ALU.is_gt, fill=0.0,
                                     base=0, pattern=[[1, E], [-1, E]], channel_multiplier=0))
            const(pool.memset(mhalf[:, :], -0.5))
            const(pool.memset(epst[:, :], EPS))
            assert made[0] == POOL_CONSTS
            pool.memset(free[:, 0:1], 0.0).then_inc(s_fin, 1)
            pool.memset(free[:, 1:2], 0.0).then_inc(s_fin, 1)
            pool.memset(free[:, 2:3], 0.0).then_inc(s_ma, 1)
            pool.memset(free[:, 3:4], 0.0).then_inc(s_ma, 1)

            def deviation(i, mv, n, rs, chain, done):
                pool.tensor_tensor(ve[:, n, :], mv[:, :, 1], epst[:, :], ALU.add).then_inc(chain, 1)
                pool.wait_ge(chain, i + 1)
                pool.tensor_tensor(rs[:, :], ve[:, n, :], mhalf[:, :], ALU.pow).then_inc(done, 1)

            def first_norm(i):
                pool.wait_ge(s_mv1, i + 1)
                deviation(i, mv1, 0, rs1, c_ln1, s_rs1)

            def residual(i):
                after(pool, s_ac, 2 * i)
                pool.wait_ge(s_y1, TP * (i + 1))
                pool.tensor_tensor(res[:, :, :], x_in[:, :, :], bot[:, :].unsqueeze(1).to_broadcast([P, TP, D]),
                                   ALU.add).then_inc(s_res, 1)

            def experts(j, t, steps=range(5)):
                n, h = (0, 1, 0, 2)[t], t % 3 % 2
                first, read = 12 * j + 4 * n, 3 * NEB * j + NEB * n
                for step in steps:
                    if step == 0:
                        pool.wait_ge(s_ma, read + 4)
                        pool.tensor_tensor(tmp[:, h, 0, :], tmp[:, h, 0, :], tmp[:, h, 1, :], ALU.add).then_inc(c_fin, 1)
                    if step == 1:
                        pool.wait_ge(s_ma, read + 6)
                        pool.tensor_tensor(tmp[:, h, 2, :], tmp[:, h, 2, :], tmp[:, h, 3, :], ALU.add).then_inc(c_fin, 1)
                    if step == 2:
                        pool.wait_ge(c_fin, first + 2)
                        pool.tensor_tensor(tmp[:, h, 0, :], tmp[:, h, 0, :], tmp[:, h, 2, :], ALU.add).then_inc(c_fin, 1)
                    if step == 3:
                        pool.wait_ge(c_fin, first + 3)
                        pool.wait_ge(s_ac, 2 * j + t // 2 + 1)
                        pool.tensor_tensor(acc[:, t, :], acc[:, t, :], tmp[:, h, 0, 0:D], ALU.add).then_inc(c_fin, 1)
                    if step == 4:
                        pool.wait_ge(c_fin, first + 4)
                        pool.tensor_tensor(acc[:, t, :], acc[:, t, :], tmp[:, h, 0, D:2 * D], ALU.add).then_inc(s_fin, 1)

            def probs_low(i, u):
                if u >= 3:
                    pool.wait_ge(s_av, 2 * TP * i + u - 2)
                pool.wait_ge(s_pf, 2 * TP * i + u + 1)
                pool.tensor_tensor(pr[:, u % 3, 1, :], pf[:, 0, :], pr[:, u % 3, 0, :], ALU.subtract).then_inc(s_pl[0], 1)

            def compare(i):
                pool.wait_ge(s_geq, i + 1)
                pool.tensor_tensor(geq[:, :, :, :].rearrange("p t a b -> p t (a b)"),
                                   geq[:, :, :, :].rearrange("p t a b -> p t (a b)"),
                                   lower[:, :, :].rearrange("p a b -> p (a b)").unsqueeze(1).to_broadcast([P, TP, E * E]),
                                   ALU.mult).then_inc(c_cmp, 1)
                pool.wait_ge(c_cmp, i + 1)
                pool.tensor_tensor(gtw[:, :, :, :], gtw[:, :, :, :], geq[:, :, :, :], ALU.add).then_inc(s_cmp, 1)

            def batch(i, with_experts, more):
                residual(i)
                if with_experts:
                    experts(i - 1, 0, range(3))
                for u in range(0, 2 * TP, 2):
                    probs_low(i, u)
                    if u == 0:
                        if with_experts:
                            experts(i - 1, 0, range(3, 5))
                        if more:
                            first_norm(i + 1)
                    elif with_experts:
                        experts(i - 1, 1, ([0], [1], [2, 3, 4])[u // 2 - 1])
                pool.wait_ge(s_mv2, i + 1)
                deviation(i, mv2, 1, rs2, c_ln2, s_rs2)
                if with_experts:
                    experts(i - 1, 3, range(1))
                compare(i)
                if with_experts:
                    experts(i - 1, 3, range(1, 5))

            first_norm(0)
            pool.wait_ge(s_bo, 2)
            batch(0, False, True)
            with pool.Fori(1, B - 1) as i:
                batch(i, True, True)
            batch(B - 1, True, False)
            for t in range(2):
                experts(B - 1, t)


_INS = ['x', 'ctx_1024', 'g_xattn', 'g_ffn', 'L0_xattn_Wq', 'L0_xattn_bq', 'L0_xattn_Wk', 'L0_xattn_bk',
        'L0_xattn_Wv', 'L0_xattn_bv', 'L0_xattn_Wo', 'L0_xattn_bo', 'L0_ffn_gate_w', 'L0_ffn_gate_b',
        'L0_ffn_expert_w', 'L0_ffn_expert_b']


def kernel(**inputs):
    import numpy as _np
    import concourse.bacc as _bacc
    from concourse import mybir as _mybir
    from concourse.bass_utils import run_bass_kernel_spmd as _run

    nc = _bacc.Bacc("TRN2", target_bir_lowering=False, num_devices=1)
    arrays, args = {}, []
    for name in _INS:
        a = _np.ascontiguousarray(inputs[name])
        arrays[f"in_{name}"] = a
        args.append(nc.dram_tensor(f"in_{name}", a.shape, _mybir.dt.from_np(a.dtype), kind="ExternalInput").ap())
    args.append(nc.dram_tensor("out_0", inputs["x"].shape, _mybir.dt.float32, kind="ExternalOutput").ap())
    flamingo_layer(nc, *args)
    return _run(nc, [arrays], core_ids=[0]).results[0]["out_0"]
```
